# Optimizing a Trainium2 kernel written in Bass

```python
import numpy as np
import jax
import jax.numpy as jnp

def _softmax(x, axis=-1):
    return jax.nn.softmax(x, axis=axis)

def _gelu(x):
    return jax.nn.gelu(x, approximate=True)

def _silu(x):
    return jax.nn.silu(x)

def _sigmoid(x):
    return jax.nn.sigmoid(x)

def _layernorm(x, axis=-1, eps=1e-05):
    m = jnp.mean(x, axis=axis, keepdims=True)
    v = jnp.var(x, axis=axis, keepdims=True)
    return (x - m) / jnp.sqrt(v + eps)

def _scatter_add(tgt, idx, src, axis=0):
    return tgt.at[idx].add(src)

def _segment_sum(src, seg, n):
    return jax.ops.segment_sum(src, seg, n)
kernel_name = 'mk_gnn_preln_d1_gnn_r8_6732b0'

def setup_inputs(seed: int=0):
    np.random.seed(seed)
    _w = jnp.asarray

    def _rec_inputs():
        import jax
        import jax.numpy as jnp
        _gk = jax.random.key(seed)
        x = -0.0003713 + 1 * jax.random.normal(jax.random.fold_in(_gk, 1), (12500, 256), jnp.float32)
        _s = jax.random.randint(jax.random.fold_in(_gk, 2), (100000,), 0, 12500, jnp.int32)
        _d = jax.random.randint(jax.random.fold_in(_gk, 3), (100000,), 0, 12500, jnp.int32)
        _loop = jnp.arange(12500, dtype=jnp.int32)
        src = jnp.concatenate([_s, _d, _loop])
        dst = jnp.concatenate([_d, _s, _loop])
        _o = jnp.argsort(dst, stable=True)
        src = src[_o]
        dst = dst[_o]
        edge_attr_128 = 9.41057e-06 + 1 * jax.random.normal(jax.random.fold_in(_gk, 11), (212500, 128), jnp.float32)
        node_vec1 = jax.random.uniform(jax.random.fold_in(_gk, 13), (12500, 1), jnp.float32, 0.0, 0.999973)
        node_vec1_n2 = jax.random.uniform(jax.random.fold_in(_gk, 14), (12500, 1), jnp.float32, 0.0, 0.999973)
        return (x, src, dst, edge_attr_128, node_vec1, node_vec1_n2)
    x, src, dst, edge_attr_128, node_vec1, node_vec1_n2 = _rec_inputs()

    def _L0_gnn_setup():
        import jax, jax.numpy as jnp
        import numpy as np
        NUM_NODES = 6250
        NUM_EDGES = 200000
        NODE_DIM = 256
        EDGE_DIM = 128
        MAX_IN_DEGREE = 512
        MAX_OUT_DEGREE = 512
        key = jax.random.key(seed)
        ks = jax.random.split(key, 12)
        x = jax.random.normal(ks[0], (NUM_NODES, NODE_DIM), dtype=jnp.float32)
        edge_index = jax.random.randint(ks[1], (2, NUM_EDGES), 0, NUM_NODES, dtype=jnp.int64 if jax.config.read('jax_enable_x64') else jnp.int32)
        edge_attr = jax.random.normal(ks[2], (NUM_EDGES, EDGE_DIM), dtype=jnp.float32)
        voronoi_values = jax.random.uniform(ks[3], (NUM_NODES, 1), dtype=jnp.float32)
        centralities = jax.random.uniform(ks[4], (NUM_NODES, 1), dtype=jnp.float32)
        z_in = jax.random.normal(ks[5], (MAX_IN_DEGREE, NODE_DIM), dtype=jnp.float32)
        z_out = jax.random.normal(ks[6], (MAX_OUT_DEGREE, NODE_DIM), dtype=jnp.float32)
        W_cent = jax.random.normal(ks[7], (1, NODE_DIM), dtype=jnp.float32) * 0.5
        b_cent = jnp.zeros((NODE_DIM,), dtype=jnp.float32)
        W_vor = jax.random.normal(ks[8], (1, NODE_DIM), dtype=jnp.float32) * 0.5
        b_vor = jnp.zeros((NODE_DIM,), dtype=jnp.float32)
        W_sum = jax.random.normal(ks[9], (EDGE_DIM, NODE_DIM), dtype=jnp.float32) * (1.0 / np.sqrt(EDGE_DIM))
        b_sum = jnp.zeros((NODE_DIM,), dtype=jnp.float32)
        return {'x': x, 'edge_index': edge_index, 'edge_attr': edge_attr, 'voronoi_values': voronoi_values, 'centralities': centralities, 'z_in': z_in, 'z_out': z_out, 'W_cent': W_cent, 'b_cent': b_cent, 'W_vor': W_vor, 'b_vor': b_vor, 'W_sum': W_sum, 'b_sum': b_sum}
    _L0_gnn_all = _L0_gnn_setup()
    _L0_gnn_in = {k: v for k, v in _L0_gnn_all.items() if k in ('z_in', 'z_out', 'W_cent', 'b_cent', 'W_vor', 'b_vor', 'W_sum', 'b_sum')}
    del _L0_gnn_all
    return {'x': x, 'src': src, 'dst': dst, 'edge_attr_128': edge_attr_128, 'node_vec1': node_vec1, 'node_vec1_n2': node_vec1_n2, 'L0_gnn_z_in': _L0_gnn_in['z_in'], 'L0_gnn_z_out': _L0_gnn_in['z_out'], 'L0_gnn_W_cent': _L0_gnn_in['W_cent'], 'L0_gnn_b_cent': _L0_gnn_in['b_cent'], 'L0_gnn_W_vor': _L0_gnn_in['W_vor'], 'L0_gnn_b_vor': _L0_gnn_in['b_vor'], 'L0_gnn_W_sum': _L0_gnn_in['W_sum'], 'L0_gnn_b_sum': _L0_gnn_in['b_sum']}

def reference(x, src, dst, edge_attr_128, node_vec1, node_vec1_n2, L0_gnn_z_in, L0_gnn_z_out, L0_gnn_W_cent, L0_gnn_b_cent, L0_gnn_W_vor, L0_gnn_b_vor, L0_gnn_W_sum, L0_gnn_b_sum):
    import jax
    import jax.numpy as jnp

    def _L0_gnn_ref(x, edge_index, edge_attr, voronoi_values, centralities, z_in, z_out, W_cent, b_cent, W_vor, b_vor, W_sum, b_sum):
        import jax, jax.numpy as jnp
        import numpy as np
        NUM_NODES = 6250
        NUM_EDGES = 200000
        NODE_DIM = 256
        EDGE_DIM = 128
        MAX_IN_DEGREE = 512
        MAX_OUT_DEGREE = 512
        num_nodes = x.shape[0]
        src = edge_index[0]
        dst = edge_index[1]
        ones = jnp.ones_like(src, dtype=jnp.int32)
        in_deg = jnp.minimum(jax.ops.segment_sum(ones, dst, num_segments=num_nodes), MAX_IN_DEGREE - 1)
        out_deg = jnp.minimum(jax.ops.segment_sum(ones, src, num_segments=num_nodes), MAX_OUT_DEGREE - 1)
        edge_proj = edge_attr @ W_sum + b_sum
        sum3d = jax.ops.segment_sum(edge_proj, src, num_segments=num_nodes)
        cent_term = jax.nn.sigmoid(centralities @ W_cent + b_cent)
        vor_term = jax.nn.sigmoid(voronoi_values @ W_vor + b_vor)
        return x + z_in[in_deg] + z_out[out_deg] + cent_term + vor_term + sum3d
    edge_index = jnp.stack([src, dst])
    h = jnp.maximum(_layernorm(x, axis=-1), 0.0)
    x = x + _L0_gnn_ref(h, edge_index, edge_attr_128, node_vec1, node_vec1_n2, L0_gnn_z_in, L0_gnn_z_out, L0_gnn_W_cent, L0_gnn_b_cent, L0_gnn_W_vor, L0_gnn_b_vor, L0_gnn_W_sum, L0_gnn_b_sum)
    return x

_drawn_inputs = setup_inputs


def setup_inputs(seed=0):
    import zlib

    import numpy as np

    out = dict(_drawn_inputs(seed))
    spreads = {'L0_gnn_b_cent': (0.0, 2.0), 'L0_gnn_b_vor': (0.0, 2.0), 'L0_gnn_b_sum': (0.0, 0.1)}
    factors = {'node_vec1': 8.0, 'node_vec1_n2': 8.0, 'L0_gnn_W_cent': 4.116, 'L0_gnn_W_vor': 4.361}
    for name, (base, spread) in spreads.items():
        noise = np.random.default_rng([zlib.crc32(name.encode()), seed]).standard_normal(out[name].shape)
        drawn = base * np.exp(spread * noise) if base else spread * noise
        out[name] = jnp.asarray(drawn.astype(out[name].dtype))
    for name, factor in factors.items():
        out[name] = (out[name] * factor).astype(out[name].dtype)
    return out
```

```python
from contextlib import ExitStack

import concourse.bass as bass
from concourse import mybir

ALU = mybir.AluOpType
ACT = mybir.ActivationFunctionType
F32 = mybir.dt.float32
BF16 = mybir.dt.bfloat16
I32 = mybir.dt.int32

P = 128
TABLES = 4
QUAD = TABLES
LOAD_TILES = 20
EDGE_SLOTS = 2
SUM_SLOTS = 3
TAIL_WINDOWS = 7
X_WINDOWS = 14
EPS = 1e-5


def gnn_kernel(nc, x, src, dst, edge, cent, vor, z_in, z_out, w_cent, b_cent, w_vor, b_vor, w_sum, b_sum,
               tables, out):
    N, D = x.shape
    E, F = edge.shape
    DEG = z_in.shape[0]
    KZ = DEG // P
    FULL = E // P
    REST = E - FULL * P
    NT = FULL + (REST > 0)
    NQ = -(-NT // QUAD)
    NW = -(-N // P)
    LASTW = N - (NW - 1) * P
    ROWS = tables[0].shape[0]
    assert F == P and ROWS == N + P and REST > 0 and FULL % LOAD_TILES == 0 and LOAD_TILES % QUAD == 0
    assert NW % TAIL_WINDOWS == 0 and NW % X_WINDOWS == 0 and DEG % P == 0 and NT % QUAD == 1
    NLOAD = FULL // LOAD_TILES
    QPL = LOAD_TILES // QUAD
    NTAIL = NW // TAIL_WINDOWS
    ZERO_COLS = ROWS * F // P // 7
    assert ZERO_COLS * 7 * P == ROWS * F

    def tiles(q):
        return range(min(QUAD, NT - q * QUAD))

    side = [[] for _ in range(NQ)]
    HIST_SLOTS = NQ // 2
    for h in range(NQ):
        side[h // 2].append(("hist", h))
    for w in range(NW):
        side[2 * w + 1].append(("stats", w))
    side[HIST_SLOTS].append(("degrees", 0))
    for w in range(NW + 1):
        side[HIST_SLOTS + 1 + 2 * w].append(("node", w))

    with ExitStack() as ctx:
        def sb(name, shape, dt=F32):
            return ctx.enter_context(nc.sbuf_tensor(name, shape, dt))

        def sem(name):
            return ctx.enter_context(nc.semaphore(name))

        base = sb("base", [P, NW, D])
        edge_ring = sb("edge_ring", [P, EDGE_SLOTS * LOAD_TILES * F])
        edge_last = sb("edge_last", [P, F])
        summed = sb("summed", [P, SUM_SLOTS, QUAD * F])
        same = sb("same", [P, 2, QUAD * P])
        index_area = sb("index_area", [P, 4 * NT])
        src_i = index_area[:, 0:NT].bitcast(I32)
        src_f = index_area[:, NT:2 * NT]
        halves = index_area[:, 2 * NT:4 * NT].bitcast(BF16)
        src_hi, src_lo, dst_hi, dst_lo = (halves[:, k * NT:(k + 1) * NT] for k in range(4))
        scratch = sb("scratch", [P, 5 * 512])
        dst_i = scratch[:, 0:NT].bitcast(I32)
        z_f = scratch[:, 0:2 * KZ * D]
        pre = scratch[:, 0:1024].rearrange("p (b n) -> p b n", b=2)
        gate = scratch[:, 1024:2048].rearrange("p (b n) -> p b n", b=2)
        normed = scratch[:, 2048:2560].rearrange("p (b n) -> p b n", b=2)
        z_parts = sb("z_parts", [P, 3, 2 * KZ * D], BF16)
        zeros = z_parts[:, :, :].rearrange("p a b -> p (a b)").bitcast(F32)[:, 0:ZERO_COLS]
        onehot = sb("onehot", [P, 2, QUAD, 2, P + NW], BF16)
        z_hot = sb("z_hot", [P, 2, 2, KZ, P], BF16)
        ident = sb("ident", [P, P])
        ident_b = sb("ident_b", [P, P], BF16)
        before = sb("before", [P, P])
        junk = sb("junk", [P, QUAD, P], BF16)
        iota_lo = sb("iota_lo", [P, P], BF16)
        iota_hi = sb("iota_hi", [P, NW], BF16)
        dummy_i = sb("dummy_i", [P, 1], I32)
        dummy = sb("dummy_row", [P, 1])
        bins = sb("bins", [P, KZ])
        earlier = sb("earlier", [P, 2, QUAD])
        divert = sb("divert", [P, 2, QUAD])
        vec_rows = sb("vec_rows", [P, 2, P])
        vec_cols = sb("vec_cols", [P, 2, NW])
        rows_b = sb("rows_b", [P, 5, D])
        w_sb = sb("w_sb", [P, D])
        stats = sb("stats", [P, 2, 6])
        meanvar = sb("meanvar", [P, NW, 2])
        rstd = sb("rstd", [P, 3, NW])
        shift = sb("shift", [P, NW])
        outdeg = sb("outdeg", [P, NW])
        degc = sb("degc", [P, 2, NW])
        pair = sb("pair", [P, 2, 2 * F])
        sumT = sb("sumT", [P, 2, P])
        tail = [edge_ring[:, 0:TAIL_WINDOWS * TABLES * F], index_area[:, 0:TAIL_WINDOWS * TABLES * F]]
        tail = [t.rearrange("p (w t f) -> p w t f", t=TABLES, f=F) for t in tail]

        bank = [ctx.enter_context(nc.psum_tensor(f"bank{i}", [P, 512], F32)) for i in range(8)]
        ps_src = bank[0:2]
        ps_sum = bank[2:4]
        ps_out_count, ps_in_count = bank[4][:, 0:NW], bank[5][:, 0:NW]
        ps_deg = [bank[6], bank[4]]
        ps_z = [bank[7], bank[5]]
        ps_sumT = bank[0:2]
        ps_y = bank[2:4]

        s_idx_in = [sem("s_src_in"), sem("s_dst_in")]
        s_const_in = sem("s_const_in")
        s_z_in = sem("s_z_in")
        s_zeroed = [sem(f"s_zeroed{t}") for t in range(TABLES)]
        s_edge = [sem(f"s_edge{i}") for i in range(EDGE_SLOTS)]
        s_edge_last = sem("s_edge_last")
        s_x = [sem(f"s_x{i}") for i in range(NW // X_WINDOWS)]
        s_scatter = [sem(f"s_scatter{t}") for t in range(TABLES)]
        s_tail = [sem(f"s_tail{i}") for i in range(2)]
        s_out = sem("s_out")
        s_made = sem("s_made")
        s_fill = sem("s_fill")
        s_cleared = sem("s_cleared")
        s_keys = sem("s_keys")
        s_chain = sem("s_chain")
        s_srow = sem("s_srow")
        s_same = sem("s_same")
        s_rank = sem("s_rank")
        s_rows = sem("s_rows")
        s_comb = sem("s_comb")
        s_evac = sem("s_evac")
        s_hot = sem("s_hot")
        s_count = sem("s_count")
        s_mean = sem("s_mean")
        s_var = sem("s_var")
        s_root = sem("s_root")
        s_deg = sem("s_deg")
        s_vec = sem("s_vec")
        s_degrow = sem("s_degrow")
        s_zhot = sem("s_zhot")
        s_z = sem("s_z")
        s_pre = sem("s_pre")
        s_norm = sem("s_norm")
        s_gate = sem("s_gate")
        s_node = sem("s_node")
        s_pair = sem("s_pair")
        s_sumT = sem("s_sumT")
        s_sumT_sb = sem("s_sumT_sb")
        s_y = sem("s_y")
        s_fin = sem("s_fin")

        def edges_of(g):
            s = g % EDGE_SLOTS
            n = LOAD_TILES * F
            return edge_ring[:, s * n:(s + 1) * n], edge[0:FULL * P, :].rearrange(
                "(p t) f -> p (t f)", p=P)[:, g * n:(g + 1) * n]

        def store(act, c):
            w0, w1 = c * TAIL_WINDOWS, (c + 1) * TAIL_WINDOWS
            act.wait_ge(s_fin, w1)
            full = min(w1, NW - 1)
            act.dma_start(out[w0 * P:full * P, :].rearrange("(w p) d -> p w d", p=P), base[:, w0:full, :]).then_inc(s_out, 16)
            if full < w1:
                act.dma_start(out[full * P:N, :], base[0:LASTW, full, :]).then_inc(s_out, 16)

        block = ctx.enter_context(nc.Block())

        @block.sync
        def _(sp):
            sp.dma_start(src_i[:, 0:FULL], src[0:FULL * P].rearrange("(p t) -> p t", p=P)).then_inc(s_idx_in[0], 16)
            sp.dma_start(dst_i[:, 0:FULL], dst[0:FULL * P].rearrange("(p t) -> p t", p=P)).then_inc(s_idx_in[1], 16)
            sp.wait_ge(s_cleared, 6)
            sp.dma_start(src_i[0:REST, FULL:NT], src[FULL * P:E].rearrange("(p t) -> p t", t=1)).then_inc(s_idx_in[0], 16)
            sp.dma_start(dst_i[0:REST, FULL:NT], dst[FULL * P:E].rearrange("(p t) -> p t", t=1)).then_inc(s_idx_in[1], 16)

            def zero(t):
                sp.dma_start(tables[t].rearrange("r f -> (r f)").rearrange("(p a c) -> p a c", p=P, a=7),
                             zeros.unsqueeze(1).to_broadcast([P, 7, ZERO_COLS])).then_inc(s_zeroed[t], 16)

            zero(0)
            a, b = edges_of(0)
            sp.dma_start(a, b).then_inc(s_edge[0], 16)
            for t in range(1, TABLES):
                zero(t)
            for g in range(1, EDGE_SLOTS):
                a, b = edges_of(g)
                sp.dma_start(a, b).then_inc(s_edge[g], 16)
            sp.dma_start(edge_last[0:REST, :], edge[FULL * P:E, :]).then_inc(s_edge_last, 16)
            for k, v in enumerate((cent, vor)):
                sp.dma_start(vec_rows[0:NW - 1, k, :], v[0:(NW - 1) * P, :].rearrange("(w p) o -> w (p o)", p=P)).then_inc(s_const_in, 16)
                sp.dma_start(vec_rows[NW - 1:NW, k, 0:LASTW], v[(NW - 1) * P:N, :].rearrange("p o -> o p")).then_inc(s_const_in, 16)
            for k, v in enumerate((w_cent, w_vor, b_cent, b_vor, b_sum)):
                row = v if k < 2 else v.rearrange("(o d) -> o d", o=1)
                sp.dma_start(rows_b[:, k, :], row[0].partition_broadcast(P)).then_inc(s_const_in, 16)
            sp.dma_start(w_sb[:, :], w_sum).then_inc(s_const_in, 16)
            sp.wait_ge(s_keys, 2)
            for k, z in enumerate((z_in, z_out)):
                sp.dma_start(z_f[:, k * KZ * D:(k + 1) * KZ * D].rearrange("p (c d) -> p c d", c=KZ),
                             z.rearrange("(c p) d -> p c d", p=P)).then_inc(s_z_in, 16)
            nx = 0
            for g in range(EDGE_SLOTS, NLOAD):
                if nx < len(s_x) and g % 3 == 2:
                    w0, w1 = nx * X_WINDOWS, (nx + 1) * X_WINDOWS
                    if w1 < NW:
                        sp.dma_start(base[:, w0:w1, :], x[w0 * P:w1 * P, :].rearrange("(w p) d -> p w d", p=P)).then_inc(s_x[nx], 16)
                    else:
                        sp.dma_start(base[:, w0:NW - 1, :], x[w0 * P:(NW - 1) * P, :].rearrange("(w p) d -> p w d", p=P)).then_inc(s_x[nx], 16)
                        sp.dma_start(base[0:LASTW, NW - 1, :], x[(NW - 1) * P:N, :]).then_inc(s_x[nx], 16)
                    nx += 1
                sp.wait_ge(s_comb, (g - EDGE_SLOTS + 1) * QPL)
                a, b = edges_of(g)
                sp.dma_start(a, b).then_inc(s_edge[g % EDGE_SLOTS], 16)
            sp.wait_ge(s_comb, NQ)
            sp.wait_ge(s_rows, NQ)
            sp.wait_ge(s_count, NQ)
            for t in range(TABLES):
                sp.wait_ge(s_scatter[t], 16 * len(range(t, NT, TABLES)))
            for c in range(NTAIL):
                if c >= 2:
                    sp.wait_ge(s_pair, (c - 1) * TAIL_WINDOWS)
                for t in range(TABLES):
                    r0 = c * TAIL_WINDOWS * P
                    sp.dma_start(tail[c % 2][:, :, t, :], tables[t][r0:r0 + TAIL_WINDOWS * P, :].rearrange(
                        "(w p) f -> p w f", p=P)).then_inc(s_tail[c % 2], 16)
            sp.wait_ge(s_out, 16 * (NTAIL + 1))

        @block.gpsimd
        def _(pool):
            g = nc.gpsimd
            g.iota(dummy_i[:, :], pattern=[[0, 1]], base=N, channel_multiplier=1).then_inc(s_made, 1)
            g.memset(ident[:, :], 0.0).then_inc(s_fill, 1)
            g.memset(before[:, :], 1.0).then_inc(s_fill, 1)
            pool.wait_ge(s_fill, 2)
            g.affine_select(out=ident[:, :], in_=ident[:, :], compare_op=ALU.not_equal, fill=1.0, base=0,
                            pattern=[[-1, P]], channel_multiplier=1).then_inc(s_made, 1)
            g.affine_select(out=before[:, :], in_=before[:, :], compare_op=ALU.is_gt, fill=0.0, base=0,
                            pattern=[[-1, P]], channel_multiplier=1).then_inc(s_made, 1)
            g.iota(iota_lo[:, :], pattern=[[1, P]], base=0, channel_multiplier=0,
                   allow_small_or_imprecise_dtypes=True).then_inc(s_made, 1)
            g.iota(iota_hi[:, :], pattern=[[P, NW]], base=0, channel_multiplier=0,
                   allow_small_or_imprecise_dtypes=True).then_inc(s_made, 1)
            g.iota(bins[:, :], pattern=[[P, KZ]], base=0, channel_multiplier=1,
                   allow_small_or_imprecise_dtypes=True).then_inc(s_made, 1)
            for q in range(NQ):
                pool.wait_ge(s_rows, q + 1)
                pool.wait_ge(s_evac, q + 1)
                for t in tiles(q):
                    if q == 0:
                        pool.wait_ge(s_zeroed[t], 16)
                    else:
                        pool.wait_ge(s_scatter[t], 16 * q)
                    c = q * QUAD + t
                    g.indirect_dma_start(tables[t][:, :], bass.IndirectOffsetOnAxis(src_i[:, c:c + 1], 0),
                                         summed[:, q % SUM_SLOTS, t * F:(t + 1) * F], None,
                                         compute_op=ALU.add).then_inc(s_scatter[t], 16)

        @block.vector
        def _(dve):
            v = nc.vector
            chained = [0]

            def link(ins):
                chained[0] += 1
                ins.then_inc(s_chain, 1)
                dve.wait_ge(s_chain, chained[0])

            v.memset(zeros, 0.0).then_inc(s_cleared, 1)
            dve.wait_ge(s_made, 1)
            v.tensor_copy(src_i[:, FULL:NT], dummy_i[:, :]).then_inc(s_cleared, 1)
            v.tensor_copy(dst_i[:, FULL:NT], dummy_i[:, :]).then_inc(s_cleared, 1)
            v.memset(edge_last[:, :], 0.0).then_inc(s_cleared, 1)
            v.memset(vec_rows[:, :, :], 0.0).then_inc(s_cleared, 1)
            v.memset(base[:, NW - 1, :], 0.0).then_inc(s_cleared, 1)
            v.tensor_copy(dummy[:, :], dummy_i[:, :])
            dve.wait_ge(s_made, 6)
            v.tensor_copy(ident_b[:, :], ident[:, :])
            for k, (whole, hi, lo) in enumerate(((src_i, src_hi, src_lo), (dst_i, dst_hi, dst_lo))):
                dve.wait_ge(s_idx_in[k], 32)
                tmp = base[:, 0:NT // D + 1, :].rearrange("p a b -> p (a b)")[:, 0:NT].bitcast(I32)
                link(v.tensor_scalar(tmp, whole, P - 1, None, ALU.bitwise_and))
                link(v.tensor_copy(lo, tmp))
                link(v.tensor_scalar(tmp, whole, -P, None, ALU.bitwise_and))
                if k == 0:
                    v.tensor_copy(src_f, src_i)
                v.tensor_copy(hi, tmp).then_inc(s_keys, 1)
                dve.wait_ge(s_keys, k + 1)

            def quad(q):
                n = len(tiles(q))
                c = q * QUAD
                dve.wait_ge(s_srow, q + 1)
                if q >= 2:
                    dve.wait_ge(s_comb, q - 1)
                if q == 0:
                    dve.wait_ge(s_keys, 2)
                v.tensor_tensor(same[:, q % 2, 0:n * P].rearrange("p (t j) -> p t j", t=n),
                                ps_src[q % 2][:, 0:n * P].rearrange("p (t j) -> p t j", t=n),
                                src_f[:, c:c + n].unsqueeze(2).to_broadcast([P, n, P]),
                                ALU.is_equal).then_inc(s_same, 1)
                dve.wait_ge(s_same, q + 1)
                for t in range(n):
                    v.tensor_tensor_reduce(out=junk[:, t, :], in0=same[:, q % 2, t * P:(t + 1) * P],
                                           in1=before[:, :], scale=1.0, scalar=0.0, op0=ALU.mult, op1=ALU.add,
                                           accum_out=earlier[:, q % 2, t:t + 1]).then_inc(s_rank, 1)

            def rows(q):
                n = len(tiles(q))
                c = q * QUAD
                dve.wait_ge(s_rank, c + n)
                if q >= 2:
                    dve.wait_ge(s_rows, q - 1)
                link(v.tensor_scalar(divert[:, q % 2, 0:n], earlier[:, q % 2, 0:n], 1.0, dummy[:, 0:1],
                                     ALU.min, ALU.mult))
                v.tensor_tensor(src_i[:, c:c + n], divert[:, q % 2, 0:n], src_f[:, c:c + n],
                                ALU.max).then_inc(s_rows, 1)

            def hist(h):
                if h >= 2:
                    dve.wait_ge(s_count, h - 1)
                for t in tiles(h):
                    c = h * QUAD + t
                    for k, (hi, lo) in enumerate(((src_hi, src_lo), (dst_hi, dst_lo))):
                        v.tensor_scalar(onehot[:, h % 2, t, k, 0:P], iota_lo[:, :], lo[:, c:c + 1], None, ALU.is_equal)
                        last = v.tensor_scalar(onehot[:, h % 2, t, k, P:P + NW], iota_hi[:, :], hi[:, c:c + 1], None, ALU.is_equal)
                last.then_inc(s_hot, 1)

            def stat(w):
                if w % X_WINDOWS == 0:
                    i = w // X_WINDOWS
                    dve.wait_ge(s_x[i], 32 if i == len(s_x) - 1 else 16)
                if w >= 2:
                    dve.wait_ge(s_mean, w - 1)
                link(v.bn_stats(stats[:, w % 2, :], base[:, w, :]))
                v.bn_aggr(meanvar[:, w, :], stats[:, w % 2, :]).then_inc(s_mean, 1)
                if w == NW - 1:
                    dve.wait_ge(s_mean, NW)
                    v.tensor_scalar(rstd[:, 0, :], meanvar[:, :, 1], EPS, None, ALU.add).then_inc(s_var, 1)

            def z_split():
                dve.wait_ge(s_z_in, 32)
                for t in range(TABLES):
                    dve.wait_ge(s_zeroed[t], 16)
                link(v.tensor_copy(z_parts[:, 0, :], z_f))
                link(v.tensor_tensor(z_f, z_f, z_parts[:, 0, :], ALU.subtract))
                link(v.tensor_copy(z_parts[:, 1, :], z_f))
                link(v.tensor_tensor(z_f, z_f, z_parts[:, 1, :], ALU.subtract))
                link(v.tensor_copy(z_parts[:, 2, :], z_f))

            def degrees():
                z_split()
                dve.wait_ge(s_count, NQ)
                v.tensor_copy(outdeg[:, :], ps_out_count)
                v.tensor_scalar(degc[:, 0, :], ps_in_count, DEG - 1.0, None, ALU.min)
                v.tensor_scalar(degc[:, 1, :], ps_out_count, DEG - 1.0, None, ALU.min)
                dve.wait_ge(s_root, 1)
                link(v.reciprocal(rstd[:, 2, :], rstd[:, 1, :]))
                v.scalar_tensor_tensor(out=shift[:, :], in0=meanvar[:, :, 0], scalar=-1.0, in1=rstd[:, 2, :],
                                       op0=ALU.mult, op1=ALU.mult)
                dve.wait_ge(s_vec, 1)
                link(v.tensor_copy(vec_cols[:, :, :], ps_deg[0][:, 0:2 * NW].rearrange("p (k w) -> p k w", k=2)))
                v.tensor_copy(divert[:, 0, 0:1], dummy[:, :]).then_inc(s_deg, 1)

            def node_args(w):
                b = w % 2
                if w >= 2:
                    dve.wait_ge(s_gate, w - 1)
                for k in range(2):
                    last = v.scalar_tensor_tensor(out=pre[:, b, k * D:(k + 1) * D], in0=rows_b[:, k, :],
                                                  scalar=vec_cols[:, k, w:w + 1], in1=rows_b[:, 2 + k, :],
                                                  op0=ALU.mult, op1=ALU.add)
                last.then_inc(s_pre, 1)
                dve.wait_ge(s_degrow, w + 1)
                if w >= 2:
                    dve.wait_ge(s_z, w - 1)
                for k in range(2):
                    last = v.tensor_tensor(z_hot[:, b, k, :, :],
                                           ps_deg[b][:, k * P:(k + 1) * P].unsqueeze(1).to_broadcast([P, KZ, P]),
                                           bins[:, :].unsqueeze(2).to_broadcast([P, KZ, P]), ALU.is_equal)
                last.then_inc(s_zhot, 1)

            def node_sum(w):
                b = w % 2
                acc = base[:, w, :]
                dve.wait_ge(s_norm, w + 1)
                link(v.tensor_tensor(acc, acc, normed[:, b, :], ALU.add))
                dve.wait_ge(s_gate, w + 1)
                link(v.tensor_tensor(acc, acc, gate[:, b, 0:D], ALU.add))
                link(v.tensor_tensor(acc, acc, gate[:, b, D:2 * D], ALU.add))
                link(v.scalar_tensor_tensor(out=acc, in0=rows_b[:, 4, :], scalar=outdeg[:, w:w + 1], in1=acc,
                                            op0=ALU.mult, op1=ALU.add))
                dve.wait_ge(s_z, w + 1)
                v.tensor_tensor(acc, ps_z[b][:, 0:D], acc, ALU.add).then_inc(s_node, 1)

            for q in range(NQ):
                quad(q)
                rows(q)
                for what, i in side[q]:
                    if what == "hist":
                        hist(i)
                    elif what == "stats":
                        stat(i)
                    elif what == "degrees":
                        degrees()
                    else:
                        if i < NW:
                            node_args(i)
                        if i > 0:
                            node_sum(i - 1)

            def finish(w):
                dve.wait_ge(s_y, w + 1)
                v.tensor_tensor(base[:, w, :], ps_y[w % 2][:, 0:D], base[:, w, :], ALU.add).then_inc(s_fin, 1)

            dve.wait_ge(s_node, NW)
            for w in range(NW):
                c = w // TAIL_WINDOWS
                dve.wait_ge(s_tail[c % 2], 16 * TABLES * (c // 2 + 1))
                if w >= 2:
                    dve.wait_ge(s_sumT, w - 1)
                part = tail[c % 2][:, w % TAIL_WINDOWS, :, :].rearrange("p t f -> p (t f)")
                v.tensor_tensor(pair[:, w % 2, :], part[:, 0:2 * F], part[:, 2 * F:4 * F], ALU.add).then_inc(s_pair, 1)
                if w >= 2:
                    finish(w - 2)
            finish(NW - 2)
            finish(NW - 1)

        @block.scalar
        def _(act):
            a = nc.scalar
            for q in range(NQ):
                n = len(tiles(q))
                act.wait_ge(s_comb, q + 1)
                if q >= SUM_SLOTS:
                    for t in range(TABLES):
                        act.wait_ge(s_scatter[t], 16 * (q - SUM_SLOTS + 1))
                a.activation(summed[:, q % SUM_SLOTS, 0:n * F], ps_sum[q % 2][:, 0:n * F], ACT.Copy).then_inc(s_evac, 1)
                for what, i in side[q]:
                    if what == "degrees":
                        act.wait_ge(s_var, 1)
                        a.activation(rstd[:, 1, :], rstd[:, 0, :], ACT.Sqrt).then_inc(s_root, 1)
                    elif what == "node" and i < NW:
                        b = i % 2
                        if i == 0:
                            act.wait_ge(s_deg, 1)
                        if i >= 2:
                            act.wait_ge(s_node, i - 1)
                        a.activation(normed[:, b, :], base[:, i, :], ACT.Relu, bias=shift[:, i:i + 1],
                                     scale=rstd[:, 2, i:i + 1]).then_inc(s_norm, 1)
                        act.wait_ge(s_pre, i + 1)
                        a.activation(gate[:, b, :], pre[:, b, :], ACT.Sigmoid).then_inc(s_gate, 1)

            for w in range(NW):
                act.wait_ge(s_sumT, w + 1)
                if w >= 2:
                    act.wait_ge(s_y, w - 1)
                a.activation(sumT[:, w % 2, :], ps_sumT[w % 2][:, 0:P], ACT.Copy).then_inc(s_sumT_sb, 1)
                c, r = divmod(w, TAIL_WINDOWS)
                if r == 3 and c > 0:
                    store(act, c - 1)
            store(act, NTAIL - 1)

        @block.tensor
        def _(pe):
            t_ = nc.tensor

            def spread(q):
                if q >= 2:
                    pe.wait_ge(s_same, q - 1)
                for t in tiles(q):
                    c = q * QUAD + t
                    for k, part in enumerate((src_hi, src_lo)):
                        last = t_.matmul(ps_src[q % 2][:, t * P:(t + 1) * P], part[:, c:c + 1].to_broadcast([P, P]),
                                         ident_b[:, :], start=(k == 0), stop=(k == 1))
                last.then_inc(s_srow, 1)

            def combine(q):
                pe.wait_ge(s_same, q + 1)
                g = q // QPL
                if g < NLOAD:
                    pe.wait_ge(s_edge[g % EDGE_SLOTS], 16 * (g // EDGE_SLOTS + 1))
                else:
                    pe.wait_ge(s_edge_last, 16)
                if q >= 2:
                    pe.wait_ge(s_evac, q - 1)
                for t in tiles(q):
                    c = q * QUAD + t
                    if c < FULL:
                        at = (g % EDGE_SLOTS) * LOAD_TILES + c % LOAD_TILES
                        row = edge_ring[:, at * F:(at + 1) * F]
                    else:
                        row = edge_last[:, :]
                    last = t_.matmul(ps_sum[q % 2][:, t * F:(t + 1) * F], same[:, q % 2, t * P:(t + 1) * P], row,
                                     start=True, stop=True)
                last.then_inc(s_comb, 1)

            def count(h):
                pe.wait_ge(s_hot, h + 1)
                for t in tiles(h):
                    for k, acc in enumerate((ps_out_count, ps_in_count)):
                        c = h * QUAD + t
                        last = t_.matmul(acc, onehot[:, h % 2, t, k, 0:P], onehot[:, h % 2, t, k, P:P + NW],
                                         start=(c == 0), stop=(c == NT - 1))
                last.then_inc(s_count, 1)

            def spread_degrees(w):
                if w >= 2:
                    pe.wait_ge(s_zhot, w - 1)
                for k in range(2):
                    last = t_.matmul(ps_deg[w % 2][:, k * P:(k + 1) * P], degc[:, k, w:w + 1].to_broadcast([P, P]),
                                     ident[:, :], start=True, stop=True)
                last.then_inc(s_degrow, 1)

            def pick_z(w):
                pe.wait_ge(s_zhot, w + 1)
                if w >= 2:
                    pe.wait_ge(s_node, w - 1)
                b, n = w % 2, 0
                for k in range(2):
                    for c in range(KZ):
                        for part in range(3):
                            at = (k * KZ + c) * D
                            last = t_.matmul(ps_z[b][:, 0:D], z_hot[:, b, k, c, :], z_parts[:, part, at:at + D],
                                             start=(n == 0), stop=(n == 6 * KZ - 1))
                            n += 1
                last.then_inc(s_z, 1)

            pe.wait_ge(s_keys, 2)
            spread(0)
            pe.wait_ge(s_const_in, 16 * 10)
            for k in range(2):
                last = t_.matmul(ps_deg[0][:, k * NW:(k + 1) * NW], vec_rows[0:NW, k, :], ident[0:NW, 0:NW],
                                 start=True, stop=True)
            last.then_inc(s_vec, 1)
            for q in range(NQ):
                if q + 1 < NQ:
                    spread(q + 1)
                combine(q)
                for what, i in side[q]:
                    if what == "hist":
                        count(i)
                    elif what == "degrees":
                        pe.wait_ge(s_deg, 1)
                        spread_degrees(0)
                    elif what == "node" and i < NW:
                        if i + 1 < NW:
                            spread_degrees(i + 1)
                        pick_z(i)

            def transpose_sum(w):
                pe.wait_ge(s_pair, w + 1)
                if w >= 2:
                    pe.wait_ge(s_sumT_sb, w - 1)
                for k in range(2):
                    last = t_.matmul(ps_sumT[w % 2][:, 0:P], pair[:, w % 2, k * F:(k + 1) * F], ident[:, :],
                                     start=(k == 0), stop=(k == 1))
                last.then_inc(s_sumT, 1)

            def project(w):
                pe.wait_ge(s_sumT_sb, w + 1)
                if w >= 2:
                    pe.wait_ge(s_fin, w - 1)
                t_.matmul(ps_y[w % 2][:, 0:D], sumT[:, w % 2, :], w_sb[:, :], start=True, stop=True).then_inc(s_y, 1)

            transpose_sum(0)
            for w in range(NW):
                if w + 1 < NW:
                    transpose_sum(w + 1)
                project(w)


_INS = ['x', 'src', 'dst', 'edge_attr_128', 'node_vec1', 'node_vec1_n2', 'L0_gnn_z_in', 'L0_gnn_z_out',
        'L0_gnn_W_cent', 'L0_gnn_b_cent', 'L0_gnn_W_vor', 'L0_gnn_b_vor', 'L0_gnn_W_sum', 'L0_gnn_b_sum']


def kernel(**inputs):
    import numpy as _np
    import concourse.bacc as _bacc
    from concourse import mybir as _mybir
    from concourse.bass_utils import run_bass_kernel_spmd as _run

    nc = _bacc.Bacc("TRN2", target_bir_lowering=False, num_devices=1)
    arrays, aps = {}, {}
    for name in _INS:
        a = _np.ascontiguousarray(inputs[name])
        arrays[f"in_{name}_dram"] = a
        aps[name] = nc.dram_tensor(f"in_{name}_dram", a.shape, _mybir.dt.from_np(a.dtype), kind="ExternalInput").ap()
    n, d = inputs['x'].shape
    f = inputs['edge_attr_128'].shape[1]
    out = nc.dram_tensor("out_0_dram", (n, d), _mybir.dt.float32, kind="ExternalOutput").ap()
    tables = [nc.dram_tensor(f"table{t}", (n + P, f), _mybir.dt.float32).ap() for t in range(TABLES)]
    gnn_kernel(nc, aps['x'], aps['src'], aps['dst'], aps['edge_attr_128'], aps['node_vec1_n2'], aps['node_vec1'],
               aps['L0_gnn_z_in'], aps['L0_gnn_z_out'], aps['L0_gnn_W_cent'], aps['L0_gnn_b_cent'],
               aps['L0_gnn_W_vor'], aps['L0_gnn_b_vor'], aps['L0_gnn_W_sum'], aps['L0_gnn_b_sum'], tables, out)
    r = _run(nc, [arrays], core_ids=[0])
    return r.results[0]["out_0_dram"]
```

```python
from contextlib import ExitStack

import concourse.bass as bass
from concourse import mybir

ALU = mybir.AluOpType
ACT = mybir.ActivationFunctionType
F32 = mybir.dt.float32
BF16 = mybir.dt.bfloat16
I32 = mybir.dt.int32

P = 128
TABLES = 5
QUAD = 4
LOAD_TILES = 10
EDGE_SLOTS = 4
SUM_SLOTS = 4
NODE_P = 125
WIDE_P = 112
TAIL_WINDOWS = 7
X_WINDOWS = 10
GROUP = 32
EPS = 1e-5


def gnn_kernel(nc, x, src, dst, edge, cent, vor, z_in, z_out, w_cent, b_cent, w_vor, b_vor, w_sum, b_sum,
               tables, out):
    N, D = x.shape
    E, F = edge.shape
    DEG = z_in.shape[0]
    KZ = DEG // P
    FULL = E // P
    REST = E - FULL * P
    NT = FULL + (REST > 0)
    NQ = -(-NT // QUAD)
    NW = N // NODE_P
    ROWS = tables[0].shape[0]
    assert N == NW * NODE_P and NODE_P <= P and NW <= P and ROWS == NW * P >= N + P and F == P
    assert REST > 0 and FULL % LOAD_TILES == 0 and DEG % P == 0
    assert NW % X_WINDOWS == 0
    NTP = NQ * QUAD
    NLOAD = FULL // LOAD_TILES
    ZERO_COPIES = 8
    ZERO_COLS = NW * F // ZERO_COPIES

    tail_sizes = [2]
    while sum(tail_sizes) < NW:
        left = NW - sum(tail_sizes)
        tail_sizes.append(min(TAIL_WINDOWS, left - 2) if left > 2 else left)
    tail_start = [sum(tail_sizes[:c]) for c in range(len(tail_sizes) + 1)]
    NTAIL = len(tail_sizes)

    table_of = [0] * 4 + [0, 1] * 4 + [0, 1, 2] * 4 + [0, 1, 2, 3] * 4
    table_of += [i % TABLES for i in range(NT - len(table_of))]
    turn = [table_of[:i].count(t) for i, t in enumerate(table_of)]

    def tiles(q):
        return range(min(QUAD, NT - q * QUAD))

    side = [[] for _ in range(NQ)]
    HIST_SLOTS = NQ // 2
    for h in range(NQ):
        side[h // 2].append(("hist", h))
    for w in range(NW):
        side[HIST_SLOTS - NW + w].append(("stats", w))
    side[HIST_SLOTS].append(("degrees", 0))
    for w in range(NW + 1):
        side[HIST_SLOTS + 1 + 2 * w].append(("node", w))
    assert not side[NQ - 1]

    with ExitStack() as ctx:
        def sb(name, shape, dt=F32):
            return ctx.enter_context(nc.sbuf_tensor(name, shape, dt))

        def sem(name):
            return ctx.enter_context(nc.semaphore(name))

        base = sb("base", [P, NW, D])
        edge_ring = sb("edge_ring", [P, EDGE_SLOTS * LOAD_TILES * F])
        edge_last = sb("edge_last", [P, F])
        summed = sb("summed", [P, SUM_SLOTS, QUAD * F])
        same = sb("same", [P, 2, QUAD * P])
        index_area = sb("index_area", [P, 4 * NTP])
        src_i = index_area[:, 0:NT].bitcast(I32)
        key_f = index_area[:, NTP:2 * NTP]
        halves = index_area[:, 2 * NTP:4 * NTP].bitcast(BF16).rearrange("p (k t) -> p k t", k=4)
        scratch = sb("scratch", [P, 5 * 512])
        dst_i = scratch[:, 0:NT].bitcast(I32)
        z_f = scratch[:, 0:2 * KZ * D]
        pre = scratch[:, 0:1024].rearrange("p (b n) -> p b n", b=2)
        gate = scratch[:, 1024:2048].rearrange("p (b n) -> p b n", b=2)
        normed = scratch[:, 2048:2560].rearrange("p (b n) -> p b n", b=2)
        z_parts = sb("z_parts", [P, 3, 2 * KZ * D], BF16)
        zeros = z_parts[:, :, :].rearrange("p a b -> p (a b)").bitcast(F32)[:, 0:ZERO_COLS]
        hot_hi = sb("hot_hi", [P, 2, P, 2, QUAD], BF16)
        hot_lo = sb("hot_lo", [P, 2, NW, 2, QUAD], BF16)
        z_hot = sb("z_hot", [P, 2, 2, KZ, NODE_P], BF16)
        ident = sb("ident", [P, P])
        ident_b = sb("ident_b", [P, P], BF16)
        weigh_bits = sb("weigh_bits", [P, P // GROUP], I32)
        look_bits = sb("look_bits", [P, P // GROUP], I32)
        weigh, look = weigh_bits[:, :].bitcast(F32), look_bits[:, :].bitcast(F32)
        seen = sb("seen", [P, 2, QUAD, P // GROUP])
        iota_hi = sb("iota_hi", [P, P, 2, QUAD], BF16)
        iota_lo = sb("iota_lo", [P, NW, 2, QUAD], BF16)
        dummy_i = sb("dummy_i", [P, 1], I32)
        dummy = sb("dummy_row", [P, 1])
        bins = sb("bins", [P, KZ])
        earlier = sb("earlier", [P, 2, QUAD])
        divert = sb("divert", [P, 2, QUAD])
        vec_cols = sb("vec_cols", [P, 2, NW])
        rows_b = sb("rows_b", [P, 5, D])
        w_sb = sb("w_sb", [P, D])
        stats = sb("stats", [P, 2, 6])
        meanvar = sb("meanvar", [P, NW, 2])
        rstd = sb("rstd", [P, 3, NW])
        shift = sb("shift", [P, NW])
        outdeg = sb("outdeg", [P, NW])
        degc = sb("degc", [P, 2, NW])
        pair = scratch[:, 0:4 * F].rearrange("p (b n) -> p b n", b=2)
        sumT = scratch[:, 4 * F:6 * F].rearrange("p (b n) -> p b n", b=2)
        tail = [edge_ring[:, 0:TAIL_WINDOWS * TABLES * F], index_area[:, 0:TAIL_WINDOWS * TABLES * F]]
        tail = [t.rearrange("p (w t f) -> p w t f", t=TABLES, f=F) for t in tail]

        bank = [ctx.enter_context(nc.psum_tensor(f"bank{i}", [P, 512], F32)) for i in range(8)]
        ps_src = bank[0:2]
        ps_sum = bank[2:4]
        ps_out_count, ps_in_count = bank[4][:, 0:NW], bank[5][:, 0:NW]
        ps_deg = [bank[6], bank[4]]
        ps_z = [bank[7], bank[5]]
        ps_seen = [b[:, 0:QUAD * (P // GROUP)].rearrange("p (t g) -> p t g", t=QUAD) for b in ps_src]
        ps_sumT = bank[0:2]
        ps_y = bank[2:4]

        s_idx_in = [sem("s_src_in"), sem("s_dst_in")]
        s_const_in = sem("s_const_in")
        s_z_in = sem("s_z_in")
        s_zeroed = [sem(f"s_zeroed{i}") for i in range(2)]
        s_edge = [sem(f"s_edge{i}") for i in range(EDGE_SLOTS)]
        s_edge_last = sem("s_edge_last")
        s_x = [sem(f"s_x{i}") for i in range(NW // X_WINDOWS)]
        s_scatter = [sem(f"s_scatter{t}") for t in range(TABLES)]
        s_tail = [sem(f"s_tail{i}") for i in range(2)]
        s_out = sem("s_out")
        s_made = sem("s_made")
        s_fill = sem("s_fill")
        s_cleared = sem("s_cleared")
        s_keys = sem("s_keys")
        s_chain = sem("s_chain")
        s_srow = sem("s_srow")
        s_same = sem("s_same")
        s_seen = sem("s_seen")
        s_rows = sem("s_rows")
        s_comb = sem("s_comb")
        s_evac = sem("s_evac")
        s_hot = sem("s_hot")
        s_count = sem("s_count")
        s_mean = sem("s_mean")
        s_var = sem("s_var")
        s_root = sem("s_root")
        s_deg = sem("s_deg")
        s_degrow = sem("s_degrow")
        s_zhot = sem("s_zhot")
        s_z = sem("s_z")
        s_pre = sem("s_pre")
        s_norm = sem("s_norm")
        s_gate = sem("s_gate")
        s_node = sem("s_node")
        s_pair = sem("s_pair")
        s_sumT = sem("s_sumT")
        s_sumT_sb = sem("s_sumT_sb")
        s_y = sem("s_y")
        s_fin = sem("s_fin")

        def load_of(w):
            return max(c for c in range(NTAIL) if tail_start[c] <= w)

        def edges_of(g):
            s = g % EDGE_SLOTS
            n = LOAD_TILES * F
            return edge_ring[:, s * n:(s + 1) * n], edge[0:FULL * P, :].rearrange(
                "(p t) f -> p (t f)", p=P)[:, g * n:(g + 1) * n]

        def by_partition(ap):
            return ap.rearrange("(p w) d -> p w d", w=NW)

        def store(act, c):
            w0, w1 = tail_start[c:c + 2]
            act.wait_ge(s_fin, w1)
            for p0, p1 in ((0, WIDE_P), (WIDE_P, NODE_P)):
                act.dma_start(by_partition(out)[p0:p1, w0:w1, :], base[p0:p1, w0:w1, :]).then_inc(s_out, 16)

        block = ctx.enter_context(nc.Block())

        @block.sync
        def _(sp):
            sp.dma_start(src_i[:, 0:FULL], src[0:FULL * P].rearrange("(p t) -> p t", p=P)).then_inc(s_idx_in[0], 16)

            def load(g):
                a, b = edges_of(g)
                sp.dma_start(a, b).then_inc(s_edge[g % EDGE_SLOTS], 16)

            load(0)
            sp.wait_ge(s_cleared, 1)
            pieces = [(t, a) for t in range(TABLES) for a in range(ZERO_COPIES)]
            for n, (t, a) in enumerate(pieces):
                if n >= 2:
                    sp.wait_ge(s_zeroed[n % 2], 16 * (n // 2))
                table = tables[t].rearrange("r f -> (r f)").rearrange("(p a c) -> p a c", p=P, a=ZERO_COPIES)
                sp.dma_start(table[:, a, :], zeros).then_inc(s_zeroed[n % 2], 16)
                if n == 1:
                    sp.dma_start(dst_i[:, 0:FULL], dst[0:FULL * P].rearrange("(p t) -> p t", p=P)).then_inc(s_idx_in[1], 16)
                if n % 8 == 7 and n // 8 + 1 < EDGE_SLOTS:
                    load(n // 8 + 1)
            sp.wait_ge(s_cleared, 4)
            sp.dma_start(edge_last[0:REST, :], edge[FULL * P:E, :]).then_inc(s_edge_last, 16)
            for k, v in enumerate((cent, vor)):
                sp.dma_start(vec_cols[0:NODE_P, k, :], v.rearrange("(p w) o -> p (w o)", w=NW)).then_inc(s_const_in, 16)
            for k, v in enumerate((w_cent, w_vor, b_cent, b_vor, b_sum)):
                row = v if k < 2 else v.rearrange("(o d) -> o d", o=1)
                sp.dma_start(rows_b[:, k, :], row[0].partition_broadcast(P)).then_inc(s_const_in, 16)
            sp.dma_start(w_sb[:, :], w_sum).then_inc(s_const_in, 16)
            sp.wait_ge(s_keys, 2)
            for k, z in enumerate((z_in, z_out)):
                sp.dma_start(z_f[:, k * KZ * D:(k + 1) * KZ * D].rearrange("p (c d) -> p c d", c=KZ),
                             z.rearrange("(c p) d -> p c d", p=P)).then_inc(s_z_in, 16)
            for g in range(EDGE_SLOTS, NLOAD):
                i, r = divmod(g, 4)
                if r == 0 and 0 < i <= len(s_x):
                    i -= 1
                    w0, w1 = i * X_WINDOWS, (i + 1) * X_WINDOWS
                    for p0, p1 in ((0, WIDE_P), (WIDE_P, NODE_P)):
                        sp.dma_start(base[p0:p1, w0:w1, :], by_partition(x)[p0:p1, w0:w1, :]).then_inc(s_x[i], 16)
                sp.wait_ge(s_comb, ((g - EDGE_SLOTS + 1) * LOAD_TILES - 1) // QUAD + 1)
                load(g)
            sp.wait_ge(s_comb, NQ)
            sp.wait_ge(s_rows, NQ)
            sp.wait_ge(s_count, NQ)
            for t in range(TABLES):
                sp.wait_ge(s_scatter[t], 16 * table_of.count(t))
            for c in range(NTAIL):
                w0, w1 = tail_start[c:c + 2]
                if c >= 2:
                    sp.wait_ge(s_sumT, tail_start[c - 1])
                for t in range(TABLES):
                    sp.dma_start(tail[c % 2][:, 0:w1 - w0, t, :], by_partition(tables[t])[:, w0:w1, :]).then_inc(s_tail[c % 2], 16)
            sp.wait_ge(s_out, 16 * 2 * NTAIL)

        @block.gpsimd
        def _(pool):
            g = nc.gpsimd
            g.iota(dummy_i[:, :], pattern=[[0, 1]], base=N, channel_multiplier=1).then_inc(s_made, 1)
            g.memset(ident[:, :], 0.0).then_inc(s_fill, 1)
            g.memset(weigh_bits[:, :], 0).then_inc(s_fill, 1)
            g.memset(look_bits[:, :], 0).then_inc(s_fill, 1)
            pool.wait_ge(s_fill, 3)
            fills = 3
            for a in range(P // GROUP):
                r = slice(a * GROUP, (a + 1) * GROUP)
                for bits, step in ((weigh_bits, -2), (look_bits, 2)):
                    g.iota(bits[r, a:a + 1], pattern=[[0, 1]], base=127 << 23,
                           channel_multiplier=step << 23).then_inc(s_fill, 1)
                    fills += 1
                    pool.wait_ge(s_fill, fills)
            g.affine_select(out=ident[:, :], in_=ident[:, :], compare_op=ALU.not_equal, fill=1.0, base=0,
                            pattern=[[-1, P]], channel_multiplier=1).then_inc(s_made, 1)
            g.iota(iota_hi[:, :, :, :], pattern=[[P, P], [0, 2 * QUAD]], base=0, channel_multiplier=0,
                   allow_small_or_imprecise_dtypes=True).then_inc(s_made, 1)
            g.iota(iota_lo[:, :, :, :], pattern=[[1, NW], [0, 2 * QUAD]], base=0, channel_multiplier=0,
                   allow_small_or_imprecise_dtypes=True).then_inc(s_made, 1)
            g.iota(bins[:, :], pattern=[[P, KZ]], base=0, channel_multiplier=1,
                   allow_small_or_imprecise_dtypes=True).then_inc(s_made, 1)
            for q in range(NQ):
                pool.wait_ge(s_rows, q + 1)
                pool.wait_ge(s_evac, q + 1)
                for i in range(len(tiles(q))):
                    c = q * QUAD + i
                    t = table_of[c]
                    if turn[c] == 0:
                        for half in s_zeroed:
                            pool.wait_ge(half, 16 * (t + 1) * ZERO_COPIES // 2)
                    else:
                        pool.wait_ge(s_scatter[t], 16 * turn[c])
                    g.indirect_dma_start(tables[t][:, :], bass.IndirectOffsetOnAxis(src_i[:, c:c + 1], 0),
                                         summed[:, q % SUM_SLOTS, i * F:(i + 1) * F], None,
                                         compute_op=ALU.add).then_inc(s_scatter[t], 16)

        @block.vector
        def _(dve):
            v = nc.vector
            chained = [0]

            def link(ins):
                chained[0] += 1
                ins.then_inc(s_chain, 1)
                dve.wait_ge(s_chain, chained[0])

            v.memset(zeros, 0.0).then_inc(s_cleared, 1)
            dve.wait_ge(s_made, 1)
            v.tensor_copy(src_i[:, FULL:NT], dummy_i[:, :]).then_inc(s_cleared, 1)
            v.tensor_copy(dst_i[:, FULL:NT], dummy_i[:, :]).then_inc(s_cleared, 1)
            v.memset(edge_last[:, :], 0.0).then_inc(s_cleared, 1)
            v.tensor_copy(dummy[:, :], dummy_i[:, :])
            dve.wait_ge(s_made, 5)
            v.tensor_copy(ident_b[:, :], ident[:, :])
            for a in range(1, P // GROUP):
                link(v.memset(look[a * GROUP:(a + 1) * GROUP, 0:a], 4.0 ** GROUP))
            work = base[:, 0:4 * (NTP // D + 1), :].rearrange("p a b -> p (a b)")
            work_i, quot, rest, over = (work[:, k * NTP:k * NTP + NT] for k in range(4))
            work_i = work_i.bitcast(I32)

            def keys(k):
                whole = (src_i, dst_i)[k]
                dve.wait_ge(s_idx_in[k], 32)
                link(v.tensor_scalar(rest, whole, -(NW - 1) / 2, 1.0 / NW, ALU.add, ALU.mult))
                link(v.tensor_copy(work_i, rest))
                link(v.tensor_copy(quot, work_i))
                link(v.scalar_tensor_tensor(out=rest, in0=quot, scalar=-float(NW), in1=whole,
                                            op0=ALU.mult, op1=ALU.add))
                link(v.tensor_scalar(over, rest, float(NW), None, ALU.is_ge))
                link(v.tensor_tensor(quot, quot, over, ALU.add))
                link(v.scalar_tensor_tensor(out=rest, in0=over, scalar=-float(NW), in1=rest,
                                            op0=ALU.mult, op1=ALU.add))
                if k == 0:
                    link(v.scalar_tensor_tensor(out=key_f[:, 0:NT], in0=quot, scalar=float(P), in1=rest,
                                                op0=ALU.mult, op1=ALU.add))
                v.tensor_copy(halves[:, 2 + k, 0:NT], rest)
                v.tensor_scalar(halves[:, k, 0:NT], quot, float(P), None, ALU.mult).then_inc(s_keys, 1)
                dve.wait_ge(s_keys, k + 1)

            keys(0)

            def mark(ins):
                chained[0] += 1
                ins.then_inc(s_chain, 1)
                return chained[0]

            def need(count):
                dve.wait_ge(s_chain, count)

            def quad(q):
                n = len(tiles(q))
                c = q * QUAD
                dve.wait_ge(s_srow, q + 1)
                if q >= 2:
                    dve.wait_ge(s_comb, q - 1)
                v.tensor_tensor(same[:, q % 2, 0:n * P].rearrange("p (t j) -> p t j", t=n),
                                ps_src[q % 2][:, 0:n * P].rearrange("p (t j) -> p t j", t=n),
                                key_f[:, c:c + n].unsqueeze(2).to_broadcast([P, n, P]),
                                ALU.is_equal).then_inc(s_same, 1)

            def rows(q):
                n, b, c = len(tiles(q)), q % 2, q * QUAD
                dve.wait_ge(s_comb, q + 1)
                v.tensor_tensor(seen[:, b, 0:n, :], ps_seen[b][:, 0:n, :],
                                look.unsqueeze(1).to_broadcast([P, n, P // GROUP]), ALU.mult).then_inc(s_seen, 1)
                yield
                dve.wait_ge(s_seen, q + 1)
                m = mark(v.tensor_reduce(earlier[:, b, 0:n], seen[:, b, 0:n, :], mybir.AxisListType.X, ALU.add))
                yield
                need(m)
                if q >= 2:
                    dve.wait_ge(s_rows, q - 1)
                m = mark(v.tensor_scalar(divert[:, b, 0:n], earlier[:, b, 0:n], 2.0, dummy[:, 0:1],
                                         ALU.is_ge, ALU.mult))
                yield
                need(m)
                v.tensor_tensor(src_i[:, c:c + n], divert[:, b, 0:n], src_i[:, c:c + n],
                                ALU.max).then_inc(s_rows, 1)

            def hist(h):
                if h >= 2:
                    dve.wait_ge(s_count, h - 1)
                n, c = len(tiles(h)), h * QUAD
                for hot, iota, k, bins_ in ((hot_hi, iota_hi, 0, P), (hot_lo, iota_lo, 2, NW)):
                    last = v.tensor_tensor(hot[:, h % 2, :, :, 0:n],
                                           halves[:, k:k + 2, c:c + n].unsqueeze(1).to_broadcast([P, bins_, 2, n]),
                                           iota[:, :, :, 0:n], ALU.is_equal)
                    if k == 0:
                        yield
                last.then_inc(s_hot, 1)
                yield

            def stat(w):
                if w % X_WINDOWS == 0:
                    i = w // X_WINDOWS
                    dve.wait_ge(s_x[i], 32)
                if w >= 2:
                    dve.wait_ge(s_mean, w - 1)
                m = mark(v.bn_stats(stats[0:NODE_P, w % 2, :], base[0:NODE_P, w, :]))
                yield
                need(m)
                v.bn_aggr(meanvar[0:NODE_P, w, :], stats[0:NODE_P, w % 2, :]).then_inc(s_mean, 1)
                yield
                if w == NW - 1:
                    dve.wait_ge(s_mean, NW)
                    v.tensor_scalar(rstd[0:NODE_P, 0, :], meanvar[0:NODE_P, :, 1], EPS, None, ALU.add).then_inc(s_var, 1)

            def z_split():
                dve.wait_ge(s_z_in, 32)
                for half in s_zeroed:
                    dve.wait_ge(half, 16 * TABLES * ZERO_COPIES // 2)
                link(v.tensor_copy(z_parts[:, 0, :], z_f))
                link(v.tensor_tensor(z_f, z_f, z_parts[:, 0, :], ALU.subtract))
                link(v.tensor_copy(z_parts[:, 1, :], z_f))
                link(v.tensor_tensor(z_f, z_f, z_parts[:, 1, :], ALU.subtract))
                link(v.tensor_copy(z_parts[:, 2, :], z_f))

            def degrees():
                z_split()
                dve.wait_ge(s_count, NQ)
                v.tensor_copy(outdeg[:, :], ps_out_count)
                v.tensor_scalar(degc[:, 0, :], ps_in_count, DEG - 1.0, None, ALU.min)
                v.tensor_scalar(degc[:, 1, :], ps_out_count, DEG - 1.0, None, ALU.min)
                dve.wait_ge(s_root, 1)
                link(v.reciprocal(rstd[0:NODE_P, 2, :], rstd[0:NODE_P, 1, :]))
                v.scalar_tensor_tensor(out=shift[0:NODE_P, :], in0=meanvar[0:NODE_P, :, 0], scalar=-1.0,
                                       in1=rstd[0:NODE_P, 2, :], op0=ALU.mult, op1=ALU.mult).then_inc(s_deg, 1)
                dve.wait_ge(s_deg, 1)
                dve.wait_ge(s_const_in, 16 * 8)

            def node_args(w):
                b = w % 2
                if w >= 2:
                    dve.wait_ge(s_gate, w - 1)
                for k in range(2):
                    last = v.scalar_tensor_tensor(out=pre[0:NODE_P, b, k * D:(k + 1) * D], in0=rows_b[0:NODE_P, k, :],
                                                  scalar=vec_cols[0:NODE_P, k, w:w + 1], in1=rows_b[0:NODE_P, 2 + k, :],
                                                  op0=ALU.mult, op1=ALU.add)
                    if k == 0:
                        yield
                last.then_inc(s_pre, 1)
                yield
                dve.wait_ge(s_degrow, w + 1)
                if w >= 2:
                    dve.wait_ge(s_z, w - 1)
                for k in range(2):
                    last = v.tensor_tensor(z_hot[:, b, k, :, :],
                                           ps_deg[b][:, k * P:k * P + NODE_P].unsqueeze(1).to_broadcast([P, KZ, NODE_P]),
                                           bins[:, :].unsqueeze(2).to_broadcast([P, KZ, NODE_P]), ALU.is_equal)
                    if k == 0:
                        yield
                last.then_inc(s_zhot, 1)
                yield

            def node_sum(w):
                b = w % 2
                acc = base[0:NODE_P, w, :]
                dve.wait_ge(s_norm, w + 1)
                m = mark(v.tensor_tensor(acc, acc, normed[0:NODE_P, b, :], ALU.add))
                dve.wait_ge(s_gate, w + 1)
                for part in (gate[0:NODE_P, b, 0:D], gate[0:NODE_P, b, D:2 * D]):
                    yield
                    need(m)
                    m = mark(v.tensor_tensor(acc, acc, part, ALU.add))
                yield
                need(m)
                m = mark(v.scalar_tensor_tensor(out=acc, in0=rows_b[0:NODE_P, 4, :], scalar=outdeg[0:NODE_P, w:w + 1],
                                                in1=acc, op0=ALU.mult, op1=ALU.add))
                yield
                need(m)
                dve.wait_ge(s_z, w + 1)
                v.tensor_tensor(acc, ps_z[b][0:NODE_P, 0:D], acc, ALU.add).then_inc(s_node, 1)
                yield

            def in_turn(*works):
                works = list(works)
                while works:
                    works = [x for x in works if next(x, "done") != "done"]

            def side_work(q):
                for what, i in side[q]:
                    if what == "hist":
                        yield from hist(i)
                    elif what == "stats":
                        yield from stat(i)
                    elif what == "degrees":
                        degrees()
                    else:
                        works = ([node_args(i)] if i < NW else []) + ([node_sum(i - 1)] if i > 0 else [])
                        while works:
                            works = [x for x in works if next(x, "done") != "done"]
                            yield

            quad(0)
            for q in range(NQ):
                if q + 1 < NQ:
                    quad(q + 1)
                if q == 0:
                    keys(1)
                in_turn(rows(q), side_work(q))

            def finish(w):
                dve.wait_ge(s_y, w + 1)
                v.tensor_tensor(base[0:NODE_P, w, :], ps_y[w % 2][0:NODE_P, 0:D], base[0:NODE_P, w, :], ALU.add).then_inc(s_fin, 1)

            dve.wait_ge(s_node, NW)
            for w in range(NW):
                c = load_of(w)
                dve.wait_ge(s_tail[c % 2], 16 * TABLES * (c // 2 + 1))
                if w >= 2:
                    dve.wait_ge(s_sumT, w - 1)
                part = tail[c % 2][:, w - tail_start[c], 0:4, :].rearrange("p t f -> p (t f)")
                v.tensor_tensor(pair[:, w % 2, :], part[:, 0:2 * F], part[:, 2 * F:4 * F], ALU.add).then_inc(s_pair, 1)
                if w >= 2:
                    finish(w - 2)
            finish(NW - 2)
            finish(NW - 1)

        @block.scalar
        def _(act):
            a = nc.scalar
            act.wait_ge(s_cleared, 3)
            for k, (v, to) in enumerate(((src, src_i), (dst, dst_i))):
                act.dma_start(to[0:REST, FULL:NT], v[FULL * P:E].rearrange("(p t) -> p t", t=1)).then_inc(s_idx_in[k], 16)
            for q in range(NQ):
                n = len(tiles(q))
                act.wait_ge(s_comb, q + 1)
                if q >= SUM_SLOTS:
                    for i in range(QUAD):
                        c = (q - SUM_SLOTS) * QUAD + i
                        act.wait_ge(s_scatter[table_of[c]], 16 * (turn[c] + 1))
                a.activation(summed[:, q % SUM_SLOTS, 0:n * F], ps_sum[q % 2][:, 0:n * F], ACT.Copy).then_inc(s_evac, 1)
                for what, i in side[q]:
                    if what == "degrees":
                        act.wait_ge(s_var, 1)
                        a.activation(rstd[0:NODE_P, 1, :], rstd[0:NODE_P, 0, :], ACT.Sqrt).then_inc(s_root, 1)
                    elif what == "node" and i < NW:
                        b = i % 2
                        if i == 0:
                            act.wait_ge(s_deg, 1)
                        if i >= 2:
                            act.wait_ge(s_node, i - 1)
                        a.activation(normed[0:NODE_P, b, :], base[0:NODE_P, i, :], ACT.Relu, bias=shift[0:NODE_P, i:i + 1],
                                     scale=rstd[0:NODE_P, 2, i:i + 1]).then_inc(s_norm, 1)
                        act.wait_ge(s_pre, i + 1)
                        a.activation(gate[0:NODE_P, b, :], pre[0:NODE_P, b, :], ACT.Sigmoid).then_inc(s_gate, 1)

            for w in range(NW):
                act.wait_ge(s_sumT, w + 1)
                if w >= 2:
                    act.wait_ge(s_y, w - 1)
                a.activation(sumT[:, w % 2, :], ps_sumT[w % 2][:, 0:P], ACT.Copy).then_inc(s_sumT_sb, 1)
                c = load_of(w)
                if c > 0 and w == tail_start[c] + 1:
                    store(act, c - 1)
            store(act, NTAIL - 1)

        @block.tensor
        def _(pe):
            t_ = nc.tensor

            def spread(q):
                if q >= 2:
                    pe.wait_ge(s_seen, q - 1)
                for t in tiles(q):
                    c = q * QUAD + t
                    for k, part in enumerate((0, 2)):
                        last = t_.matmul(ps_src[q % 2][:, t * P:(t + 1) * P],
                                         halves[:, part, c:c + 1].to_broadcast([P, P]),
                                         ident_b[:, :], start=(k == 0), stop=(k == 1))
                last.then_inc(s_srow, 1)

            def combine(q):
                pe.wait_ge(s_same, q + 1)
                if q >= 2:
                    pe.wait_ge(s_evac, q - 1)
                for t in tiles(q):
                    c = q * QUAD + t
                    if c < FULL:
                        g = c // LOAD_TILES
                        if t == 0 or c % LOAD_TILES == 0:
                            pe.wait_ge(s_edge[g % EDGE_SLOTS], 16 * (g // EDGE_SLOTS + 1))
                        at = (g % EDGE_SLOTS) * LOAD_TILES + c % LOAD_TILES
                        row = edge_ring[:, at * F:(at + 1) * F]
                    else:
                        pe.wait_ge(s_edge_last, 16)
                        row = edge_last[:, :]
                    t_.matmul(ps_sum[q % 2][:, t * F:(t + 1) * F], same[:, q % 2, t * P:(t + 1) * P], row,
                              start=True, stop=True)
                    last = t_.matmul(ps_seen[q % 2][:, t, :], same[:, q % 2, t * P:(t + 1) * P], weigh,
                                     start=True, stop=True)
                last.then_inc(s_comb, 1)

            def count(h):
                pe.wait_ge(s_hot, h + 1)
                for t in tiles(h):
                    for k, acc in enumerate((ps_out_count, ps_in_count)):
                        c = h * QUAD + t
                        last = t_.matmul(acc, hot_hi[:, h % 2, :, k, t], hot_lo[:, h % 2, :, k, t],
                                         start=(c == 0), stop=(c == NT - 1))
                last.then_inc(s_count, 1)

            def spread_degrees(w):
                if w >= 2:
                    pe.wait_ge(s_zhot, w - 1)
                for k in range(2):
                    last = t_.matmul(ps_deg[w % 2][:, k * P:k * P + NODE_P], degc[:, k, w:w + 1].to_broadcast([P, P]),
                                     ident[:, 0:NODE_P], start=True, stop=True)
                last.then_inc(s_degrow, 1)

            def pick_z(w):
                pe.wait_ge(s_zhot, w + 1)
                if w >= 2:
                    pe.wait_ge(s_node, w - 1)
                b, n = w % 2, 0
                for k in range(2):
                    for c in range(KZ):
                        for part in range(3):
                            at = (k * KZ + c) * D
                            last = t_.matmul(ps_z[b][0:NODE_P, 0:D], z_hot[:, b, k, c, :], z_parts[:, part, at:at + D],
                                             start=(n == 0), stop=(n == 6 * KZ - 1))
                            n += 1
                last.then_inc(s_z, 1)

            pe.wait_ge(s_keys, 1)
            pe.wait_ge(s_made, 5)
            spread(0)
            spread(1)
            for q in range(NQ):
                combine(q)
                for what, i in side[q - 1] if q > 0 else ():
                    if what == "hist":
                        count(i)
                    elif what == "degrees":
                        pe.wait_ge(s_deg, 1)
                        spread_degrees(0)
                    elif what == "node" and i < NW:
                        if i + 1 < NW:
                            spread_degrees(i + 1)
                        pick_z(i)
                if q + 2 < NQ:
                    spread(q + 2)

            def transpose_sum(w):
                pe.wait_ge(s_pair, w + 1)
                if w >= 2:
                    pe.wait_ge(s_sumT_sb, w - 1)
                c = load_of(w)
                parts = [pair[:, w % 2, 0:F], pair[:, w % 2, F:2 * F]]
                parts += [tail[c % 2][:, w - tail_start[c], t, :] for t in range(4, TABLES)]
                for k, part in enumerate(parts):
                    last = t_.matmul(ps_sumT[w % 2][:, 0:P], part, ident[:, :],
                                     start=(k == 0), stop=(k == len(parts) - 1))
                last.then_inc(s_sumT, 1)

            def project(w):
                pe.wait_ge(s_sumT_sb, w + 1)
                if w >= 2:
                    pe.wait_ge(s_fin, w - 1)
                t_.matmul(ps_y[w % 2][0:NODE_P, 0:D], sumT[:, w % 2, 0:NODE_P], w_sb[:, :], start=True, stop=True).then_inc(s_y, 1)

            transpose_sum(0)
            for w in range(NW):
                if w + 1 < NW:
                    transpose_sum(w + 1)
                project(w)


_INS = ['x', 'src', 'dst', 'edge_attr_128', 'node_vec1', 'node_vec1_n2', 'L0_gnn_z_in', 'L0_gnn_z_out',
        'L0_gnn_W_cent', 'L0_gnn_b_cent', 'L0_gnn_W_vor', 'L0_gnn_b_vor', 'L0_gnn_W_sum', 'L0_gnn_b_sum']


def kernel(**inputs):
    import numpy as _np
    import concourse.bacc as _bacc
    from concourse import mybir as _mybir
    from concourse.bass_utils import run_bass_kernel_spmd as _run

    nc = _bacc.Bacc("TRN2", target_bir_lowering=False, num_devices=1)
    arrays, aps = {}, {}
    for name in _INS:
        a = _np.ascontiguousarray(inputs[name])
        arrays[f"in_{name}_dram"] = a
        aps[name] = nc.dram_tensor(f"in_{name}_dram", a.shape, _mybir.dt.from_np(a.dtype), kind="ExternalInput").ap()
    n, d = inputs['x'].shape
    f = inputs['edge_attr_128'].shape[1]
    out = nc.dram_tensor("out_0_dram", (n, d), _mybir.dt.float32, kind="ExternalOutput").ap()
    tables = [nc.dram_tensor(f"table{t}", (n // NODE_P * P, f), _mybir.dt.float32).ap() for t in range(TABLES)]
    gnn_kernel(nc, aps['x'], aps['src'], aps['dst'], aps['edge_attr_128'], aps['node_vec1_n2'], aps['node_vec1'],
               aps['L0_gnn_z_in'], aps['L0_gnn_z_out'], aps['L0_gnn_W_cent'], aps['L0_gnn_b_cent'],
               aps['L0_gnn_W_vor'], aps['L0_gnn_b_vor'], aps['L0_gnn_W_sum'], aps['L0_gnn_b_sum'], tables, out)
    r = _run(nc, [arrays], core_ids=[0])
    return r.results[0]["out_0_dram"]
```

```python
from contextlib import ExitStack
from functools import partial

import concourse.bass as bass
from concourse import mybir

ALU = mybir.AluOpType
ACT = mybir.ActivationFunctionType
F32 = mybir.dt.float32
BF16 = mybir.dt.bfloat16
F16 = mybir.dt.float16
I32 = mybir.dt.int32

P = 128
TABLES = 3
PAIR = 2
QUAD = 4
LOAD_TILES = 10
EDGE_SLOTS = 4
SUM_SLOTS = 4
NODE_P = 125
WIDE_P = 112
TAIL_WINDOWS = 6
X_WINDOWS = 5
ZEROING = 3
HEAD = 64
GROUP = 32
EPS = 1e-5


def gnn_kernel(nc, x, src, dst, edge, cent, vor, z_in, z_out, w_cent, b_cent, w_vor, b_vor, w_sum, b_sum,
               tables, out):
    N, D = x.shape
    E, F = edge.shape
    DEG = z_in.shape[0]
    KZ = DEG // P
    FULL = E // P
    REST = E - FULL * P
    NT = FULL + (REST > 0)
    NQ = -(-NT // QUAD)
    NW = N // NODE_P
    ROWS = tables[0].shape[0]
    assert N == NW * NODE_P and NODE_P <= P and NW <= P and ROWS == NW * P >= N + PAIR * P and F == P
    assert NT % QUAD == 1 and REST > 0 and FULL % LOAD_TILES == 0 and DEG % P == 0
    assert NW % X_WINDOWS == 0 and DEG <= 2048
    NTP = NQ * QUAD
    NLOAD = FULL // LOAD_TILES
    ZERO_COPIES = 16
    ZERO_COLS = NW * F // ZERO_COPIES

    tail_sizes = [2]
    while sum(tail_sizes) < NW:
        left = NW - sum(tail_sizes)
        tail_sizes.append(min(TAIL_WINDOWS, left - 2) if left > 2 else left)
    tail_start = [sum(tail_sizes[:c]) for c in range(len(tail_sizes) + 1)]
    NTAIL = len(tail_sizes)

    NP = -(-NT // PAIR)
    table_of = [0] * 4 + [1, 0] * 3
    table_of += [k % TABLES for k in range(NP - len(table_of))]
    tiles_of = [min(PAIR, NT - PAIR * k) for k in range(NP)]
    turn = [sum(n for t, n in zip(table_of[:k], tiles_of) if t == table_of[k]) for k in range(NP)]

    def tiles(q):
        return range(min(QUAD, NT - q * QUAD))

    key_chunks = [(0, 0, HEAD), (0, HEAD, NTP // 2), (0, NTP // 2, NT), (1, 0, NTP // 2), (1, NTP // 2, NT)]
    KEYS = len(key_chunks)

    side = [[] for _ in range(NQ)]
    for i in range(1, KEYS):
        side[i - 1].append(("keys", i))
    HIST_SLOTS = KEYS - 1 + NQ // 2
    for h in range(NQ):
        side[KEYS - 1 + h // 2].append(("hist", h))
    for w in range(NW):
        side[HIST_SLOTS - NW + w].append(("stats", w))
    side[HIST_SLOTS].append(("degrees", 0))
    for w in range(NW + 1):
        side[HIST_SLOTS + 1 + 2 * w].append(("node", w))
    assert not side[NQ - 1]

    with ExitStack() as ctx:
        def sb(name, shape, dt=F32):
            return ctx.enter_context(nc.sbuf_tensor(name, shape, dt))

        def sem(name):
            return ctx.enter_context(nc.semaphore(name))

        base = sb("base", [P, NW, D])
        edge_ring = sb("edge_ring", [P, EDGE_SLOTS * LOAD_TILES * F])
        edge_last = sb("edge_last", [P, F])
        summed = sb("summed", [P, SUM_SLOTS, QUAD * F])
        same = sb("same", [P, 2, QUAD * P])
        same_b = sb("same_b", [P, 2, QUAD * P], BF16)
        cross = sb("cross", [P, 2, QUAD // PAIR, P])
        matches = sb("matches", [P, QUAD // PAIR, P], BF16)
        index_area = sb("index_area", [P, 4 * NTP])
        src_i = index_area[:, 0:NT].bitcast(I32)
        key_f = index_area[:, NTP:2 * NTP]
        halves = index_area[:, 2 * NTP:4 * NTP].bitcast(BF16).rearrange("p (k t) -> p k t", k=4)
        scratch = sb("scratch", [P, 5 * 512])
        dst_i = scratch[:, 0:NT].bitcast(I32)
        z_f = scratch[:, 0:2 * KZ * D]
        pre = scratch[:, 0:1024].rearrange("p (b n) -> p b n", b=2)
        gate = scratch[:, 1024:2048].rearrange("p (b n) -> p b n", b=2)
        normed = scratch[:, 2048:2560].rearrange("p (b n) -> p b n", b=2)
        z_parts = sb("z_parts", [P, 3, 2 * KZ * D], BF16)
        zeros = z_parts[:, :, :].rearrange("p a b -> p (a b)").bitcast(F32)[:, 0:ZERO_COLS]
        hot_hi = sb("hot_hi", [P, 2, P, 2, QUAD], BF16)
        hot_lo = sb("hot_lo", [P, 2, NW, 2, QUAD], BF16)
        z_hot = hot_hi[:, :, :, :, :].rearrange("p b h k t -> p (b h k t)")[:, 0:4 * KZ * NODE_P].rearrange(
            "p (b i k n) -> p b i k n", b=2, i=2, k=KZ)
        ident = sb("ident", [P, P])
        ident_b = sb("ident_b", [P, P], BF16)
        ident_h = sb("ident_h", [P, P], F16)
        weigh_bits = sb("weigh_bits", [P, P // GROUP], I32)
        look_bits = sb("look_bits", [P, P // GROUP], I32)
        weigh, look = weigh_bits[:, :].bitcast(F32), look_bits[:, :].bitcast(F32)
        weigh_b = sb("weigh_b", [P, P // GROUP], BF16)
        seen = sb("seen", [P, 2, QUAD, P // GROUP + 1])
        iota_hi = sb("iota_hi", [P, P, 2, QUAD], BF16)
        iota_lo = sb("iota_lo", [P, NW, 2, QUAD], BF16)
        dummy_i = sb("dummy_i", [P, 1], I32)
        dummy = sb("dummy_row", [P, QUAD])
        bins = sb("bins", [P, KZ])
        earlier = sb("earlier", [P, 2, QUAD])
        divert = sb("divert", [P, 2, QUAD])
        vec_cols = sb("vec_cols", [P, 2, NW])
        rows_b = sb("rows_b", [P, 5, D])
        w_sb = sb("w_sb", [P, D])
        stats = sb("stats", [P, 2, 6])
        meanvar = sb("meanvar", [P, NW, 2])
        rstd = sb("rstd", [P, 3, NW])
        shift = sb("shift", [P, NW])
        outdeg = sb("outdeg", [P, NW])
        degc = sb("degc", [P, 2, NW], F16)
        pair = scratch[:, 0:2 * F].rearrange("p (b n) -> p b n", b=2)
        sumT = scratch[:, 4 * F:6 * F].rearrange("p (b n) -> p b n", b=2)
        tail_cols = TAIL_WINDOWS * TABLES * F
        tail = [area[:, i * tail_cols:(i + 1) * tail_cols].rearrange("p (w t f) -> p w t f", t=TABLES, f=F)
                for i in range(2) for area in (edge_ring, index_area)]
        TAIL_SLOTS = len(tail)

        bank = [ctx.enter_context(nc.psum_tensor(f"bank{i}", [P, 512], F32)) for i in range(8)]
        ps_src = bank[0:2]
        ps_sum = bank[2:4]
        ps_out_count, ps_in_count = bank[4][:, 0:NW], bank[5][:, 0:NW]
        ps_deg = [bank[6], bank[4]]
        ps_z = [bank[7], bank[5]]
        ps_seen = [b[:, 0:QUAD * (P // GROUP)].rearrange("p (t g) -> p t g", t=QUAD) for b in ps_src]
        ps_sumT = bank[0:2]
        ps_y = bank[2:4]

        s_idx_in = [sem("s_src_in"), sem("s_dst_in")]
        s_const_in = sem("s_const_in")
        s_z_in = sem("s_z_in")
        s_zeroed = [sem(f"s_zeroed{i}") for i in range(ZEROING)]
        s_edge = [sem(f"s_edge{i}") for i in range(EDGE_SLOTS)]
        s_edge_last = sem("s_edge_last")
        s_x = [sem(f"s_x{i}") for i in range(NW // X_WINDOWS)]
        s_scatter = [sem(f"s_scatter{t}") for t in range(TABLES)]
        s_tail = [sem(f"s_tail{i}") for i in range(TAIL_SLOTS)]
        s_out = sem("s_out")
        s_made = sem("s_made")
        s_fill = sem("s_fill")
        s_cleared = sem("s_cleared")
        s_keys = sem("s_keys")
        s_chain = sem("s_chain")
        s_srow = sem("s_srow")
        s_same = sem("s_same")
        s_same_b = sem("s_same_b")
        s_cross = sem("s_cross")
        s_matched = sem("s_matched")
        s_seen = sem("s_seen")
        s_rows = sem("s_rows")
        s_comb = sem("s_comb")
        s_evac = sem("s_evac")
        s_hot = sem("s_hot")
        s_count = sem("s_count")
        s_mean = sem("s_mean")
        s_var = sem("s_var")
        s_root = sem("s_root")
        s_deg = sem("s_deg")
        s_degrow = sem("s_degrow")
        s_zhot = sem("s_zhot")
        s_z = sem("s_z")
        s_pre = sem("s_pre")
        s_norm = sem("s_norm")
        s_gate = sem("s_gate")
        s_node = sem("s_node")
        s_pair = sem("s_pair")
        s_sumT = sem("s_sumT")
        s_sumT_sb = sem("s_sumT_sb")
        s_y = sem("s_y")
        s_fin = sem("s_fin")

        def load_of(w):
            return max(c for c in range(NTAIL) if tail_start[c] <= w)

        def edges_of(g):
            s = g % EDGE_SLOTS
            n = LOAD_TILES * F
            return edge_ring[:, s * n:(s + 1) * n], edge[0:FULL * P, :].rearrange(
                "(p t) f -> p (t f)", p=P)[:, g * n:(g + 1) * n]

        def by_partition(ap):
            return ap.rearrange("(p w) d -> p w d", w=NW)

        def store(act, c):
            w0, w1 = tail_start[c:c + 2]
            act.wait_ge(s_fin, w1)
            for p0, p1 in ((0, WIDE_P), (WIDE_P, NODE_P)):
                act.dma_start(by_partition(out)[p0:p1, w0:w1, :], base[p0:p1, w0:w1, :]).then_inc(s_out, 16)

        block = ctx.enter_context(nc.Block())

        @block.sync
        def _(sp):
            sp.dma_start(src_i[:, 0:FULL], src[0:FULL * P].rearrange("(p t) -> p t", p=P)).then_inc(s_idx_in[0], 16)

            def load(g):
                a, b = edges_of(g)
                sp.dma_start(a, b).then_inc(s_edge[g % EDGE_SLOTS], 16)

            def feed(g):
                if g >= EDGE_SLOTS:
                    sp.wait_ge(s_comb, ((g - EDGE_SLOTS + 1) * LOAD_TILES - 1) // QUAD + 1)
                load(g)

            load(0)
            sp.wait_ge(s_cleared, 1)
            pieces = [(t, a) for t in range(TABLES) for a in range(ZERO_COPIES)]
            early = 0
            for n, (t, a) in enumerate(pieces):
                if n >= ZEROING:
                    sp.wait_ge(s_zeroed[n % ZEROING], 16 * (n // ZEROING))
                table = tables[t].rearrange("r f -> (r f)").rearrange("(p a c) -> p a c", p=P, a=ZERO_COPIES)
                sp.dma_start(table[:, a, :], zeros).then_inc(s_zeroed[n % ZEROING], 16)
                if n == ZERO_COPIES - 1:
                    sp.dma_start(dst_i[:, 0:FULL], dst[0:FULL * P].rearrange("(p t) -> p t", p=P)).then_inc(s_idx_in[1], 16)
                if n >= ZERO_COPIES - 1 and (n + 1) % (ZERO_COPIES // 2) == 0:
                    early += 1
                    feed(early)

            def constants():
                sp.wait_ge(s_cleared, 4)
                sp.dma_start(edge_last[0:REST, :], edge[FULL * P:E, :]).then_inc(s_edge_last, 16)
                for k, v in enumerate((cent, vor)):
                    sp.dma_start(vec_cols[0:NODE_P, k, :], v.rearrange("(p w) o -> p (w o)", w=NW)).then_inc(s_const_in, 16)
                for k, v in enumerate((w_cent, w_vor, b_cent, b_vor, b_sum)):
                    row = v if k < 2 else v.rearrange("(o d) -> o d", o=1)
                    sp.dma_start(rows_b[:, k, :], row[0].partition_broadcast(P)).then_inc(s_const_in, 16)
                sp.dma_start(w_sb[:, :], w_sum).then_inc(s_const_in, 16)

            def z_tables():
                sp.wait_ge(s_keys, KEYS)
                for k, z in enumerate((z_in, z_out)):
                    sp.dma_start(z_f[:, k * KZ * D:(k + 1) * KZ * D].rearrange("p (c d) -> p c d", c=KZ),
                                 z.rearrange("(c p) d -> p c d", p=P)).then_inc(s_z_in, 16)

            def x_windows(i):
                sp.wait_ge(s_keys, KEYS)
                w0, w1 = i * X_WINDOWS, (i + 1) * X_WINDOWS
                for p0, p1 in ((0, WIDE_P), (WIDE_P, NODE_P)):
                    sp.dma_start(base[p0:p1, w0:w1, :], by_partition(x)[p0:p1, w0:w1, :]).then_inc(s_x[i], 16)

            later = [z_tables, constants] + [partial(x_windows, i) for i in range(len(s_x))]
            for g in range(early + 1, NLOAD):
                feed(g)
                if g % 2 == 0 and later:
                    later.pop(0)()
            sp.wait_ge(s_comb, NQ)
            sp.wait_ge(s_rows, NQ)
            sp.wait_ge(s_count, NQ)
            for c in range(NTAIL):
                w0, w1 = tail_start[c:c + 2]
                if c >= TAIL_SLOTS:
                    sp.wait_ge(s_sumT, tail_start[c - TAIL_SLOTS + 1])
                for t in range(TABLES):
                    if c == 0:
                        sp.wait_ge(s_scatter[t], 16 * sum(n for k, n in enumerate(tiles_of) if table_of[k] == t))
                    sp.dma_start(tail[c % TAIL_SLOTS][:, 0:w1 - w0, t, :],
                                 by_partition(tables[t])[:, w0:w1, :]).then_inc(s_tail[c % TAIL_SLOTS], 16)
            sp.wait_ge(s_out, 16 * 2 * NTAIL)

        @block.gpsimd
        def _(pool):
            g = nc.gpsimd
            g.iota(dummy_i[:, :], pattern=[[0, 1]], base=N, channel_multiplier=1).then_inc(s_made, 1)
            g.memset(ident[:, :], 0.0).then_inc(s_fill, 1)
            g.memset(weigh_bits[:, :], 0).then_inc(s_fill, 1)
            g.memset(look_bits[:, :], 0).then_inc(s_fill, 1)
            pool.wait_ge(s_fill, 3)
            fills = 3
            for a in range(P // GROUP):
                r = slice(a * GROUP, (a + 1) * GROUP)
                for bits, step in ((weigh_bits, -2), (look_bits, 2)):
                    g.iota(bits[r, a:a + 1], pattern=[[0, 1]], base=127 << 23,
                           channel_multiplier=step << 23).then_inc(s_fill, 1)
                    fills += 1
                    pool.wait_ge(s_fill, fills)
            g.affine_select(out=ident[:, :], in_=ident[:, :], compare_op=ALU.not_equal, fill=1.0, base=0,
                            pattern=[[-1, P]], channel_multiplier=1).then_inc(s_made, 1)
            g.iota(iota_hi[:, :, :, :], pattern=[[P, P], [0, 2 * QUAD]], base=0, channel_multiplier=0,
                   allow_small_or_imprecise_dtypes=True).then_inc(s_made, 1)
            g.iota(iota_lo[:, :, :, :], pattern=[[1, NW], [0, 2 * QUAD]], base=0, channel_multiplier=0,
                   allow_small_or_imprecise_dtypes=True).then_inc(s_made, 1)
            g.iota(bins[:, :], pattern=[[P, KZ]], base=0, channel_multiplier=1,
                   allow_small_or_imprecise_dtypes=True).then_inc(s_made, 1)
            for q in range(NQ):
                pool.wait_ge(s_rows, q + 1)
                pool.wait_ge(s_evac, q + 1)
                for i in range(len(tiles(q))):
                    c = q * QUAD + i
                    k = c // PAIR
                    t = table_of[k]
                    if c % PAIR == 0 and turn[k] == 0:
                        for j, zeroed in enumerate(s_zeroed):
                            pool.wait_ge(zeroed, 16 * len(range(j, (t + 1) * ZERO_COPIES, ZEROING)))
                    elif c % PAIR == 0:
                        pool.wait_ge(s_scatter[t], 16 * turn[k])
                    g.indirect_dma_start(tables[t][:, :], bass.IndirectOffsetOnAxis(src_i[:, c:c + 1], 0),
                                         summed[:, q % SUM_SLOTS, i * F:(i + 1) * F], None,
                                         compute_op=ALU.add).then_inc(s_scatter[t], 16)

        @block.vector
        def _(dve):
            v = nc.vector
            chained = [0]

            def link(ins):
                chained[0] += 1
                ins.then_inc(s_chain, 1)
                dve.wait_ge(s_chain, chained[0])

            v.memset(zeros, 0.0).then_inc(s_cleared, 1)
            dve.wait_ge(s_made, 1)
            v.tensor_copy(src_i[:, FULL:NT], dummy_i[:, :]).then_inc(s_cleared, 1)
            v.tensor_copy(dst_i[:, FULL:NT], dummy_i[:, :]).then_inc(s_cleared, 1)
            v.memset(edge_last[:, :], 0.0).then_inc(s_cleared, 1)
            for t in range(QUAD):
                v.tensor_scalar(dummy[:, t:t + 1], dummy_i[:, :], float(t % PAIR * P), None, ALU.add)
            v.memset(seen[:, :, :, P // GROUP:], 0.0)
            dve.wait_ge(s_made, 5)
            v.tensor_copy(ident_b[:, :], ident[:, :])
            v.tensor_copy(ident_h[:, :], ident[:, :])
            v.tensor_copy(weigh_b[:, :], weigh)
            for a in range(1, P // GROUP):
                link(v.memset(look[a * GROUP:(a + 1) * GROUP, 0:a], 4.0 ** GROUP))
            work = base[:, 0:4 * (NTP // D + 1), :].rearrange("p a b -> p (a b)")

            def mark(ins):
                chained[0] += 1
                ins.then_inc(s_chain, 1)
                return chained[0]

            def need(count):
                dve.wait_ge(s_chain, count)

            def keys(i):
                k, c0, c1 = key_chunks[i]
                whole = (src_i, dst_i)[k][:, c0:c1]
                quot, rest, over = (work[:, j * NTP + c0:j * NTP + c1] for j in range(3))
                work_i = work[:, 3 * NTP + c0:3 * NTP + c1].bitcast(I32)
                dve.wait_ge(s_idx_in[k], 32)
                steps = [lambda: v.tensor_scalar(rest, whole, -(NW - 1) / 2, 1.0 / NW, ALU.add, ALU.mult),
                         lambda: v.tensor_copy(work_i, rest),
                         lambda: v.tensor_copy(quot, work_i),
                         lambda: v.scalar_tensor_tensor(out=rest, in0=quot, scalar=-float(NW), in1=whole,
                                                        op0=ALU.mult, op1=ALU.add),
                         lambda: v.tensor_scalar(over, rest, float(NW), None, ALU.is_ge),
                         lambda: v.tensor_tensor(quot, quot, over, ALU.add),
                         lambda: v.scalar_tensor_tensor(out=rest, in0=over, scalar=-float(NW), in1=rest,
                                                        op0=ALU.mult, op1=ALU.add)]
                if k == 0:
                    steps.append(lambda: v.scalar_tensor_tensor(out=key_f[:, c0:c1], in0=quot, scalar=float(P),
                                                                in1=rest, op0=ALU.mult, op1=ALU.add))
                for step in steps:
                    m = mark(step())
                    yield
                    need(m)
                v.tensor_copy(halves[:, 2 + k, c0:c1], rest)
                yield
                v.tensor_scalar(halves[:, k, c0:c1], quot, float(P), None, ALU.mult).then_inc(s_keys, 1)
                yield
                dve.wait_ge(s_keys, i + 1)

            for _ in keys(0):
                pass

            def quad(q):
                n = len(tiles(q))
                c = q * QUAD
                dve.wait_ge(s_srow, q + 1)
                if q >= 2:
                    dve.wait_ge(s_comb, q - 1)
                v.tensor_tensor(same[:, q % 2, 0:n * P].rearrange("p (t j) -> p t j", t=n),
                                ps_src[q % 2][:, 0:n * P].rearrange("p (t j) -> p t j", t=n),
                                key_f[:, c:c + n].unsqueeze(2).to_broadcast([P, n, P]),
                                ALU.is_equal).then_inc(s_same, 1)
                m = n // PAIR
                if m:
                    if q >= 2:
                        dve.wait_ge(s_matched, q - 1)
                    second = ps_src[q % 2][:, 0:m * PAIR * P].rearrange("p (k t j) -> p k t j", k=m, t=PAIR)[:, :, 1, :]
                    first = key_f[:, c:c + m * PAIR].rearrange("p (k t) -> p k t", t=PAIR)[:, :, 0:1]
                    v.tensor_tensor(cross[:, q % 2, 0:m, :], second, first.to_broadcast([P, m, P]),
                                    ALU.is_equal).then_inc(s_cross, 1)

            def rows(q):
                n, b, c = len(tiles(q)), q % 2, q * QUAD
                dve.wait_ge(s_comb, q + 1)
                v.tensor_tensor(seen[:, b, 0:n, 0:P // GROUP], ps_seen[b][:, 0:n, :],
                                look.unsqueeze(1).to_broadcast([P, n, P // GROUP]), ALU.mult).then_inc(s_seen, 1)
                yield
                dve.wait_ge(s_seen, q + 1)
                if n >= PAIR:
                    dve.wait_ge(s_matched, q + 1)
                looks = P // GROUP + (n >= PAIR)
                m = mark(v.tensor_reduce(earlier[:, b, 0:n], seen[:, b, 0:n, 0:looks], mybir.AxisListType.X, ALU.add))
                yield
                need(m)
                if q >= 2:
                    dve.wait_ge(s_rows, q - 1)
                m = mark(v.scalar_tensor_tensor(out=divert[:, b, 0:n], in0=earlier[:, b, 0:n], scalar=2.0,
                                                in1=dummy[:, 0:n], op0=ALU.is_ge, op1=ALU.mult))
                yield
                need(m)
                v.tensor_tensor(src_i[:, c:c + n], divert[:, b, 0:n], src_i[:, c:c + n],
                                ALU.max).then_inc(s_rows, 1)

            def hist(h):
                if h >= 2:
                    dve.wait_ge(s_count, h - 1)
                n, c = len(tiles(h)), h * QUAD
                for hot, iota, k, bins_ in ((hot_hi, iota_hi, 0, P), (hot_lo, iota_lo, 2, NW)):
                    last = v.tensor_tensor(hot[:, h % 2, :, :, 0:n],
                                           halves[:, k:k + 2, c:c + n].unsqueeze(1).to_broadcast([P, bins_, 2, n]),
                                           iota[:, :, :, 0:n], ALU.is_equal)
                    if k == 0:
                        yield
                last.then_inc(s_hot, 1)
                yield

            def stat(w):
                if w % X_WINDOWS == 0:
                    i = w // X_WINDOWS
                    dve.wait_ge(s_x[i], 32)
                if w >= 2:
                    dve.wait_ge(s_mean, w - 1)
                m = mark(v.bn_stats(stats[0:NODE_P, w % 2, :], base[0:NODE_P, w, :]))
                yield
                need(m)
                v.bn_aggr(meanvar[0:NODE_P, w, :], stats[0:NODE_P, w % 2, :]).then_inc(s_mean, 1)
                yield
                if w == NW - 1:
                    dve.wait_ge(s_mean, NW)
                    v.tensor_scalar(rstd[0:NODE_P, 0, :], meanvar[0:NODE_P, :, 1], EPS, None, ALU.add).then_inc(s_var, 1)

            def z_split():
                dve.wait_ge(s_z_in, 32)
                for i, zeroed in enumerate(s_zeroed):
                    dve.wait_ge(zeroed, 16 * len(range(i, TABLES * ZERO_COPIES, ZEROING)))
                link(v.tensor_copy(z_parts[:, 0, :], z_f))
                link(v.tensor_tensor(z_f, z_f, z_parts[:, 0, :], ALU.subtract))
                link(v.tensor_copy(z_parts[:, 1, :], z_f))
                link(v.tensor_tensor(z_f, z_f, z_parts[:, 1, :], ALU.subtract))
                link(v.tensor_copy(z_parts[:, 2, :], z_f))

            def degrees():
                z_split()
                dve.wait_ge(s_count, NQ)
                v.tensor_copy(outdeg[:, :], ps_out_count)
                v.tensor_scalar(degc[:, 0, :], ps_in_count, DEG - 1.0, None, ALU.min)
                v.tensor_scalar(degc[:, 1, :], ps_out_count, DEG - 1.0, None, ALU.min)
                dve.wait_ge(s_root, 1)
                link(v.reciprocal(rstd[0:NODE_P, 2, :], rstd[0:NODE_P, 1, :]))
                v.scalar_tensor_tensor(out=shift[0:NODE_P, :], in0=meanvar[0:NODE_P, :, 0], scalar=-1.0,
                                       in1=rstd[0:NODE_P, 2, :], op0=ALU.mult, op1=ALU.mult).then_inc(s_deg, 1)
                dve.wait_ge(s_deg, 1)
                dve.wait_ge(s_const_in, 16 * 8)

            def node_args(w):
                b = w % 2
                if w >= 2:
                    dve.wait_ge(s_gate, w - 1)
                for k in range(2):
                    last = v.scalar_tensor_tensor(out=pre[0:NODE_P, b, k * D:(k + 1) * D], in0=rows_b[0:NODE_P, k, :],
                                                  scalar=vec_cols[0:NODE_P, k, w:w + 1], in1=rows_b[0:NODE_P, 2 + k, :],
                                                  op0=ALU.mult, op1=ALU.add)
                    if k == 0:
                        yield
                last.then_inc(s_pre, 1)
                yield
                dve.wait_ge(s_degrow, w + 1)
                if w >= 2:
                    dve.wait_ge(s_z, w - 1)
                for k in range(2):
                    last = v.tensor_tensor(z_hot[:, b, k, :, :],
                                           ps_deg[b][:, k * P:k * P + NODE_P].unsqueeze(1).to_broadcast([P, KZ, NODE_P]),
                                           bins[:, :].unsqueeze(2).to_broadcast([P, KZ, NODE_P]), ALU.is_equal)
                    if k == 0:
                        yield
                last.then_inc(s_zhot, 1)
                yield

            def node_sum(w):
                b = w % 2
                acc = base[0:NODE_P, w, :]
                dve.wait_ge(s_norm, w + 1)
                m = mark(v.tensor_tensor(acc, acc, normed[0:NODE_P, b, :], ALU.add))
                dve.wait_ge(s_gate, w + 1)
                for part in (gate[0:NODE_P, b, 0:D], gate[0:NODE_P, b, D:2 * D]):
                    yield
                    need(m)
                    m = mark(v.tensor_tensor(acc, acc, part, ALU.add))
                yield
                need(m)
                m = mark(v.scalar_tensor_tensor(out=acc, in0=rows_b[0:NODE_P, 4, :], scalar=outdeg[0:NODE_P, w:w + 1],
                                                in1=acc, op0=ALU.mult, op1=ALU.add))
                yield
                need(m)
                dve.wait_ge(s_z, w + 1)
                v.tensor_tensor(acc, ps_z[b][0:NODE_P, 0:D], acc, ALU.add).then_inc(s_node, 1)
                yield

            def in_turn(*works):
                works = list(works)
                while works:
                    works = [x for x in works if next(x, "done") != "done"]

            def side_work(q):
                for what, i in side[q]:
                    if what == "keys":
                        yield from keys(i)
                    elif what == "hist":
                        yield from hist(i)
                    elif what == "stats":
                        yield from stat(i)
                    elif what == "degrees":
                        degrees()
                    else:
                        works = ([node_args(i)] if i < NW else []) + ([node_sum(i - 1)] if i > 0 else [])
                        while works:
                            works = [x for x in works if next(x, "done") != "done"]
                            yield

            quad(0)
            for q in range(NQ):
                if q + 1 < NQ:
                    quad(q + 1)
                in_turn(rows(q), side_work(q))

            def finish(w):
                dve.wait_ge(s_y, w + 1)
                v.tensor_tensor(base[0:NODE_P, w, :], ps_y[w % 2][0:NODE_P, 0:D], base[0:NODE_P, w, :], ALU.add).then_inc(s_fin, 1)

            dve.wait_ge(s_node, NW)
            for w in range(NW):
                c = load_of(w)
                dve.wait_ge(s_tail[c % TAIL_SLOTS], 16 * TABLES * (c // TAIL_SLOTS + 1))
                if w >= 2:
                    dve.wait_ge(s_sumT, w - 1)
                part = tail[c % TAIL_SLOTS][:, w - tail_start[c], :, :]
                v.tensor_tensor(pair[:, w % 2, :], part[:, 0, :], part[:, 1, :], ALU.add).then_inc(s_pair, 1)
                if w >= 2:
                    finish(w - 2)
            finish(NW - 2)
            finish(NW - 1)

        @block.scalar
        def _(act):
            a = nc.scalar
            act.wait_ge(s_cleared, 3)
            for k, (v, to) in enumerate(((src, src_i), (dst, dst_i))):
                act.dma_start(to[0:REST, FULL:NT], v[FULL * P:E].rearrange("(p t) -> p t", t=1)).then_inc(s_idx_in[k], 16)

            def cast(q):
                n = len(tiles(q))
                act.wait_ge(s_same, q + 1)
                if q >= 2:
                    act.wait_ge(s_comb, q - 1)
                a.activation(same_b[:, q % 2, 0:n * P], same[:, q % 2, 0:n * P], ACT.Copy).then_inc(s_same_b, 1)

            def match(q):
                act.wait_ge(s_cross, q + 1)
                if q >= 2:
                    act.wait_ge(s_rows, q - 1)
                if q >= 1:
                    act.wait_ge(s_matched, q)
                m = len(tiles(q)) // PAIR
                for k in range(m):
                    last = a.activation(matches[:, k, :], cross[:, q % 2, k, :], ACT.Copy, scale=2.0,
                                        accum_out=seen[:, q % 2, PAIR * k, P // GROUP:])
                last.then_inc(s_matched, 1)

            cast(0)
            match(0)
            for q in range(NQ):
                n = len(tiles(q))
                if q + 1 < NQ:
                    cast(q + 1)
                    if len(tiles(q + 1)) >= PAIR:
                        match(q + 1)
                act.wait_ge(s_comb, q + 1)
                if q >= SUM_SLOTS:
                    for k in range((q - SUM_SLOTS) * QUAD // PAIR, (q - SUM_SLOTS + 1) * QUAD // PAIR):
                        act.wait_ge(s_scatter[table_of[k]], 16 * (turn[k] + tiles_of[k]))
                a.activation(summed[:, q % SUM_SLOTS, 0:n * F], ps_sum[q % 2][:, 0:n * F], ACT.Copy).then_inc(s_evac, 1)
                for what, i in side[q]:
                    if what == "degrees":
                        act.wait_ge(s_var, 1)
                        a.activation(rstd[0:NODE_P, 1, :], rstd[0:NODE_P, 0, :], ACT.Sqrt).then_inc(s_root, 1)
                    elif what == "node" and i < NW:
                        b = i % 2
                        if i == 0:
                            act.wait_ge(s_deg, 1)
                        if i >= 2:
                            act.wait_ge(s_node, i - 1)
                        a.activation(normed[0:NODE_P, b, :], base[0:NODE_P, i, :], ACT.Relu, bias=shift[0:NODE_P, i:i + 1],
                                     scale=rstd[0:NODE_P, 2, i:i + 1]).then_inc(s_norm, 1)
                        act.wait_ge(s_pre, i + 1)
                        a.activation(gate[0:NODE_P, b, :], pre[0:NODE_P, b, :], ACT.Sigmoid).then_inc(s_gate, 1)

            for w in range(NW):
                act.wait_ge(s_sumT, w + 1)
                if w >= 2:
                    act.wait_ge(s_y, w - 1)
                a.activation(sumT[:, w % 2, :], ps_sumT[w % 2][:, 0:P], ACT.Copy).then_inc(s_sumT_sb, 1)
                c = load_of(w)
                if c > 0 and w == tail_start[c] + 1:
                    store(act, c - 1)
            store(act, NTAIL - 1)

        @block.tensor
        def _(pe):
            t_ = nc.tensor

            def spread(q):
                ready = max(i + 1 for i, (k, c0, _) in enumerate(key_chunks) if k == 0 and c0 <= tiles(q)[-1] + q * QUAD)
                pe.wait_ge(s_keys, ready)
                if q >= 2:
                    pe.wait_ge(s_seen, q - 1)
                for t in tiles(q):
                    c = q * QUAD + t
                    for k, part in enumerate((0, 2)):
                        last = t_.matmul(ps_src[q % 2][:, t * P:(t + 1) * P],
                                         halves[:, part, c:c + 1].to_broadcast([P, P]),
                                         ident_b[:, :], start=(k == 0), stop=(k == 1))
                last.then_inc(s_srow, 1)

            def combine(q):
                pe.wait_ge(s_same, q + 1)
                if len(tiles(q)) >= PAIR:
                    pe.wait_ge(s_cross, q + 1)
                if q >= 2:
                    pe.wait_ge(s_evac, q - 1)
                for t in tiles(q):
                    c = q * QUAD + t
                    if c < FULL:
                        g = c // LOAD_TILES
                        if t == 0 or c % LOAD_TILES == 0:
                            pe.wait_ge(s_edge[g % EDGE_SLOTS], 16 * (g // EDGE_SLOTS + 1))
                        at = (g % EDGE_SLOTS) * LOAD_TILES + c % LOAD_TILES
                        row = edge_ring[:, at * F:(at + 1) * F]
                    else:
                        pe.wait_ge(s_edge_last, 16)
                        row = edge_last[:, :]
                    second = t % PAIR == 1
                    if second:
                        t_.matmul(ps_sum[q % 2][:, t * F:(t + 1) * F], cross[:, q % 2, t // PAIR, :], first_row,
                                  start=True, stop=False)
                    first_row = row
                    t_.matmul(ps_sum[q % 2][:, t * F:(t + 1) * F], same[:, q % 2, t * P:(t + 1) * P], row,
                              start=not second, stop=True)
                pe.wait_ge(s_same_b, q + 1)
                for t in tiles(q):
                    last = t_.matmul(ps_seen[q % 2][:, t, :], same_b[:, q % 2, t * P:(t + 1) * P], weigh_b[:, :],
                                     start=True, stop=True)
                last.then_inc(s_comb, 1)

            def count(h):
                pe.wait_ge(s_hot, h + 1)
                for t in tiles(h):
                    for k, acc in enumerate((ps_out_count, ps_in_count)):
                        c = h * QUAD + t
                        last = t_.matmul(acc, hot_hi[:, h % 2, :, k, t], hot_lo[:, h % 2, :, k, t],
                                         start=(c == 0), stop=(c == NT - 1))
                last.then_inc(s_count, 1)

            def spread_degrees(w):
                if w >= 2:
                    pe.wait_ge(s_zhot, w - 1)
                for k in range(2):
                    last = t_.matmul(ps_deg[w % 2][:, k * P:k * P + NODE_P], degc[:, k, w:w + 1].to_broadcast([P, P]),
                                     ident_h[:, 0:NODE_P], start=True, stop=True)
                last.then_inc(s_degrow, 1)

            def pick_z(w):
                pe.wait_ge(s_zhot, w + 1)
                if w >= 2:
                    pe.wait_ge(s_node, w - 1)
                b, n = w % 2, 0
                for k in range(2):
                    for c in range(KZ):
                        for part in range(3):
                            at = (k * KZ + c) * D
                            last = t_.matmul(ps_z[b][0:NODE_P, 0:D], z_hot[:, b, k, c, :], z_parts[:, part, at:at + D],
                                             start=(n == 0), stop=(n == 6 * KZ - 1))
                            n += 1
                last.then_inc(s_z, 1)

            pe.wait_ge(s_made, 5)
            spread(0)
            spread(1)
            for q in range(NQ):
                combine(q)
                for what, i in side[q - 1] if q > 0 else ():
                    if what == "hist":
                        count(i)
                    elif what == "degrees":
                        pe.wait_ge(s_deg, 1)
                        spread_degrees(0)
                    elif what == "node" and i < NW:
                        if i + 1 < NW:
                            spread_degrees(i + 1)
                        pick_z(i)
                if q + 2 < NQ:
                    spread(q + 2)

            def transpose_sum(w):
                pe.wait_ge(s_pair, w + 1)
                if w >= 2:
                    pe.wait_ge(s_sumT_sb, w - 1)
                c = load_of(w)
                parts = [pair[:, w % 2, :]] + [tail[c % TAIL_SLOTS][:, w - tail_start[c], t, :] for t in range(2, TABLES)]
                for k, part in enumerate(parts):
                    last = t_.matmul(ps_sumT[w % 2][:, 0:P], part, ident[:, :],
                                     start=(k == 0), stop=(k == len(parts) - 1))
                last.then_inc(s_sumT, 1)

            def project(w):
                pe.wait_ge(s_sumT_sb, w + 1)
                if w >= 2:
                    pe.wait_ge(s_fin, w - 1)
                t_.matmul(ps_y[w % 2][0:NODE_P, 0:D], sumT[:, w % 2, 0:NODE_P], w_sb[:, :], start=True, stop=True).then_inc(s_y, 1)

            transpose_sum(0)
            for w in range(NW):
                if w + 1 < NW:
                    transpose_sum(w + 1)
                project(w)


_INS = ['x', 'src', 'dst', 'edge_attr_128', 'node_vec1', 'node_vec1_n2', 'L0_gnn_z_in', 'L0_gnn_z_out',
        'L0_gnn_W_cent', 'L0_gnn_b_cent', 'L0_gnn_W_vor', 'L0_gnn_b_vor', 'L0_gnn_W_sum', 'L0_gnn_b_sum']


def kernel(**inputs):
    import numpy as _np
    import concourse.bacc as _bacc
    from concourse import mybir as _mybir
    from concourse.bass_utils import run_bass_kernel_spmd as _run

    nc = _bacc.Bacc("TRN2", target_bir_lowering=False, num_devices=1)
    arrays, aps = {}, {}
    for name in _INS:
        a = _np.ascontiguousarray(inputs[name])
        arrays[f"in_{name}_dram"] = a
        aps[name] = nc.dram_tensor(f"in_{name}_dram", a.shape, _mybir.dt.from_np(a.dtype), kind="ExternalInput").ap()
    n, d = inputs['x'].shape
    f = inputs['edge_attr_128'].shape[1]
    out = nc.dram_tensor("out_0_dram", (n, d), _mybir.dt.float32, kind="ExternalOutput").ap()
    tables = [nc.dram_tensor(f"table{t}", (n // NODE_P * P, f), _mybir.dt.float32).ap() for t in range(TABLES)]
    gnn_kernel(nc, aps['x'], aps['src'], aps['dst'], aps['edge_attr_128'], aps['node_vec1_n2'], aps['node_vec1'],
               aps['L0_gnn_z_in'], aps['L0_gnn_z_out'], aps['L0_gnn_W_cent'], aps['L0_gnn_b_cent'],
               aps['L0_gnn_W_vor'], aps['L0_gnn_b_vor'], aps['L0_gnn_W_sum'], aps['L0_gnn_b_sum'], tables, out)
    r = _run(nc, [arrays], core_ids=[0])
    return r.results[0]["out_0_dram"]
```
